# Optimizing a Trainium2 kernel written in Bass

```python
import numpy as np
import jax
import jax.numpy as jnp

def _softmax(x, axis=-1):
    return jax.nn.softmax(x, axis=axis)

def _gelu(x):
    return jax.nn.gelu(x, approximate=True)

def _silu(x):
    return jax.nn.silu(x)

def _sigmoid(x):
    return jax.nn.sigmoid(x)

def _layernorm(x, axis=-1, eps=1e-05):
    m = jnp.mean(x, axis=axis, keepdims=True)
    v = jnp.var(x, axis=axis, keepdims=True)
    return (x - m) / jnp.sqrt(v + eps)

def _scatter_add(tgt, idx, src, axis=0):
    return tgt.at[idx].add(src)

def _segment_sum(src, seg, n):
    return jax.ops.segment_sum(src, seg, n)
kernel_name = 'mk_flamingo_gated_d2_seqx_r4_7deb95'

def setup_inputs(seed: int=0):
    np.random.seed(seed)
    _w = jnp.asarray

    def _rec_inputs():
        import jax
        import jax.numpy as jnp
        _rk = jax.random.key(seed)
        x = 7.22e-05 + 1 * jax.random.normal(jax.random.fold_in(_rk, 1), (8, 256, 256), jnp.float32)
        _lenS = 256 - jax.random.randint(jax.random.fold_in(_rk, 7), (8,), 0, max(1, 256 // 4) + 1, jnp.int32)
        _lenS2 = 256 - jax.random.randint(jax.random.fold_in(_rk, 8), (8,), 0, max(1, 256 // 4) + 1, jnp.int32)
        _ctx_1024P = jax.random.normal(jax.random.fold_in(_rk, 11), (8, 16, 256), jnp.float32)
        _ctx_1024c = jax.random.dirichlet(jax.random.fold_in(_rk, 511), 0.3 * jnp.ones((16,), jnp.float32), (8, 256))
        _ctx_1024t = jnp.einsum('bsk,bkd->bsd', _ctx_1024c, _ctx_1024P)
        _ctx_1024t = _ctx_1024t * jax.lax.rsqrt(jnp.mean(jnp.square(_ctx_1024t)) + 1e-12) * 0.953939
        ctx_1024 = 4.13588e-05 + 0.999923 * (_ctx_1024t + 0.3 * jax.random.normal(jax.random.fold_in(_rk, 611), (8, 256, 256), jnp.float32))
        _g = jax.random.normal(jax.random.fold_in(_rk, 9001), (2, 2), jnp.float32)
        _g = jnp.sign(_g) * jnp.maximum(jnp.abs(_g), 1.0) + (_g == 0) * 1.0
        g_xattn = _g[0]
        g_ffn = _g[1]
        return (x, ctx_1024, g_xattn, g_ffn)
    x, ctx_1024, g_xattn, g_ffn = _rec_inputs()

    def _L0_xattn_setup():
        import math
        import jax, jax.numpy as jnp
        import numpy as np
        EMB_DIM = 256
        CFG_N_HEADS = 16
        N_HEADS = CFG_N_HEADS if CFG_N_HEADS >= EMB_DIM else 1
        key = jax.random.key(seed)
        ks = jax.random.split(key, 11)
        B, T, C = (4, 512, EMB_DIM)
        s = 1.0 / math.sqrt(C)
        return {'q': jax.random.normal(ks[0], (B, T, C), jnp.float32), 'k': jax.random.normal(ks[1], (B, T, C), jnp.float32), 'v': jax.random.normal(ks[2], (B, T, C), jnp.float32), 'Wq': jax.random.normal(ks[3], (C, C), jnp.float32) * s, 'bq': jax.random.normal(ks[4], (C,), jnp.float32) * s, 'Wk': jax.random.normal(ks[5], (C, C), jnp.float32) * s, 'bk': jax.random.normal(ks[6], (C,), jnp.float32) * s, 'Wv': jax.random.normal(ks[7], (C, C), jnp.float32) * s, 'bv': jax.random.normal(ks[8], (C,), jnp.float32) * s, 'Wff': jax.random.normal(ks[9], (C, C), jnp.float32) * s, 'bff': jax.random.normal(ks[10], (C,), jnp.float32) * s}
    _L0_xattn_all = _L0_xattn_setup()
    _L0_xattn_in = {k: v for k, v in _L0_xattn_all.items() if k in ('Wq', 'bq', 'Wk', 'bk', 'Wv', 'bv', 'Wff', 'bff')}
    del _L0_xattn_all

    def _L0_ffn_setup():
        import jax, jax.numpy as jnp
        import numpy as np
        E = 8
        TOP_K = 2
        CAP_FACTOR = 1.25
        MIN_CAP = 4
        SCORE_SCALE = 1.0

        def _ffn(x, w1, b1, w2, b2):
            return jax.nn.gelu(x @ w1 + b1, approximate=False) @ w2 + b2
        key = jax.random.key(seed)
        ks = jax.random.split(key, 6)
        B, S, D, I = (4, 512, 256, 1024)
        std = 0.02
        return {'x': jax.random.normal(ks[0], (B, S, D), jnp.float32), 'Wr': jax.random.normal(ks[1], (E, D), jnp.float32) * std, 'W1': jax.random.normal(ks[2], (E, D, I), jnp.float32) * std, 'b1': jnp.zeros((E, I), jnp.float32), 'W2': jax.random.normal(ks[3], (E, I, D), jnp.float32) * std, 'b2': jnp.zeros((E, D), jnp.float32), 'fw1': jax.random.normal(ks[4], (D, I), jnp.float32) * std, 'fb1': jnp.zeros((I,), jnp.float32), 'fw2': jax.random.normal(ks[5], (I, D), jnp.float32) * std, 'fb2': jnp.zeros((D,), jnp.float32)}
    _L0_ffn_all = _L0_ffn_setup()
    _L0_ffn_in = {k: v for k, v in _L0_ffn_all.items() if k in ('Wr', 'W1', 'b1', 'W2', 'b2', 'fw1', 'fb1', 'fw2', 'fb2')}
    del _L0_ffn_all

    def _L1_xattn_setup():
        import jax, jax.numpy as jnp
        import numpy as np
        EMBED_DIM = 256
        NUM_HEADS = 16
        HEAD_DIM = EMBED_DIM // NUM_HEADS
        SEG_LENS = [256, 512, 1024]
        DIL_RATIOS = [1, 2, 4]
        NEG = -100000000.0

        def _branch(q, k, v, sl, dr, L):
            B = q.shape[0]
            H, D = (NUM_HEADS, HEAD_DIM)
            sl = min(sl, L)
            pad = -L % sl
            if pad:
                pw = ((0, 0), (0, pad), (0, 0), (0, 0))
                q, k, v = (jnp.pad(q, pw), jnp.pad(k, pw), jnp.pad(v, pw))
            n = (L + pad) // sl
            qs = q.reshape(B * n, sl, H, D)
            ks = k.reshape(B * n, sl, H, D)
            vs = v.reshape(B * n, sl, H, D)
            hg = H // dr
            g = sl // dr
            grp = jnp.arange(H) // hg
            pos = jnp.arange(g)[:, None] * dr + grp[None]
            hidx = jnp.arange(H)[None, :]
            sp = lambda x: x[:, pos, hidx, :]
            qd, kd, vd = (sp(qs), sp(ks), sp(vs))
            scores = jnp.einsum('bqhd,bkhd->bhqk', qd, kd) * D ** (-0.5)
            mask = jnp.tril(jnp.ones((g, g), bool))
            scores = jnp.where(mask, scores, -jnp.inf)
            lse = jax.nn.logsumexp(scores, axis=-1)
            o = jnp.einsum('bhqk,bkhd->bqhd', jnp.exp(scores - lse[..., None]), vd)
            hcol = jnp.arange(H)[:, None]
            od = jnp.zeros((B * n, H, sl, D), o.dtype).at[:, hcol, pos.T].set(o.transpose(0, 2, 1, 3))
            ld = jnp.zeros((B * n, H, sl), lse.dtype).at[:, hcol, pos.T].set(lse)
            ld = jnp.where(ld == 0.0, NEG, ld)
            od = od.reshape(B, n, H, sl, D).transpose(0, 2, 1, 3, 4)
            od = od.reshape(B, H, n * sl, D)[:, :, :L]
            ld = ld.reshape(B, n, H, sl).transpose(0, 2, 1, 3).reshape(B, H, n * sl)[:, :, :L]
            return (od, ld)
        root = jax.random.key(seed)
        ks = jax.random.split(root, 12)
        B, L, E = (1, 1024, EMBED_DIM)
        s = 0.02
        return {'query': jax.random.normal(ks[0], (B, L, E), jnp.float32), 'key': jax.random.normal(ks[1], (B, L, E), jnp.float32), 'value': jax.random.normal(ks[2], (B, L, E), jnp.float32), 'Wq': jax.random.normal(ks[3], (E, E), jnp.float32) * s, 'bq': jnp.zeros((E,), jnp.float32), 'Wk': jax.random.normal(ks[4], (E, E), jnp.float32) * s, 'bk': jnp.zeros((E,), jnp.float32), 'Wv': jax.random.normal(ks[5], (E, E), jnp.float32) * s, 'bv': jnp.zeros((E,), jnp.float32), 'Wo': jax.random.normal(ks[6], (E, E), jnp.float32) * s, 'bo': jnp.zeros((E,), jnp.float32)}
    _L1_xattn_all = _L1_xattn_setup()
    _L1_xattn_in = {k: v for k, v in _L1_xattn_all.items() if k in ('Wq', 'bq', 'Wk', 'bk', 'Wv', 'bv', 'Wo', 'bo')}
    del _L1_xattn_all

    def _L1_ffn_setup():
        import jax, jax.numpy as jnp
        import numpy as np
        B, S, H = (4, 512, 256)
        E = 8
        GS = 2
        NG = E // GS
        F = int(H * 4 * (2.0 / 3.0))
        key = jax.random.key(seed)
        ks = jax.random.split(key, 7)
        sc_h = 1.0 / np.sqrt(H)
        sc_f = 1.0 / np.sqrt(F)
        return {'x': jax.random.normal(ks[0], (B, S, H), dtype=jnp.float32), 'Wr': jax.random.normal(ks[1], (H, E), dtype=jnp.float32) * sc_h, 'br': jnp.zeros((E,), dtype=jnp.float32), 'W_up': jax.random.normal(ks[2], (NG, H, F), dtype=jnp.float32) * sc_h, 'b_up': jax.random.normal(ks[3], (NG, F), dtype=jnp.float32) * 0.01, 'W_down': jax.random.normal(ks[4], (E, F, H), dtype=jnp.float32) * sc_f, 'b_down': jax.random.normal(ks[5], (E, H), dtype=jnp.float32) * 0.01}
    _L1_ffn_all = _L1_ffn_setup()
    _L1_ffn_in = {k: v for k, v in _L1_ffn_all.items() if k in ('Wr', 'br', 'W_up', 'b_up', 'W_down', 'b_down')}
    del _L1_ffn_all
    return {'x': x, 'ctx_1024': ctx_1024, 'g_xattn': g_xattn, 'g_ffn': g_ffn, 'L0_xattn_Wq': _L0_xattn_in['Wq'], 'L0_xattn_bq': _L0_xattn_in['bq'], 'L0_xattn_Wk': _L0_xattn_in['Wk'], 'L0_xattn_bk': _L0_xattn_in['bk'], 'L0_xattn_Wv': _L0_xattn_in['Wv'], 'L0_xattn_bv': _L0_xattn_in['bv'], 'L0_xattn_Wff': _L0_xattn_in['Wff'], 'L0_xattn_bff': _L0_xattn_in['bff'], 'L0_ffn_Wr': _L0_ffn_in['Wr'], 'L0_ffn_W1': _L0_ffn_in['W1'], 'L0_ffn_b1': _L0_ffn_in['b1'], 'L0_ffn_W2': _L0_ffn_in['W2'], 'L0_ffn_b2': _L0_ffn_in['b2'], 'L0_ffn_fw1': _L0_ffn_in['fw1'], 'L0_ffn_fb1': _L0_ffn_in['fb1'], 'L0_ffn_fw2': _L0_ffn_in['fw2'], 'L0_ffn_fb2': _L0_ffn_in['fb2'], 'L1_xattn_Wq': _L1_xattn_in['Wq'], 'L1_xattn_bq': _L1_xattn_in['bq'], 'L1_xattn_Wk': _L1_xattn_in['Wk'], 'L1_xattn_bk': _L1_xattn_in['bk'], 'L1_xattn_Wv': _L1_xattn_in['Wv'], 'L1_xattn_bv': _L1_xattn_in['bv'], 'L1_xattn_Wo': _L1_xattn_in['Wo'], 'L1_xattn_bo': _L1_xattn_in['bo'], 'L1_ffn_Wr': _L1_ffn_in['Wr'], 'L1_ffn_br': _L1_ffn_in['br'], 'L1_ffn_W_up': _L1_ffn_in['W_up'], 'L1_ffn_b_up': _L1_ffn_in['b_up'], 'L1_ffn_W_down': _L1_ffn_in['W_down'], 'L1_ffn_b_down': _L1_ffn_in['b_down']}

def reference(x, ctx_1024, g_xattn, g_ffn, L0_xattn_Wq, L0_xattn_bq, L0_xattn_Wk, L0_xattn_bk, L0_xattn_Wv, L0_xattn_bv, L0_xattn_Wff, L0_xattn_bff, L0_ffn_Wr, L0_ffn_W1, L0_ffn_b1, L0_ffn_W2, L0_ffn_b2, L0_ffn_fw1, L0_ffn_fb1, L0_ffn_fw2, L0_ffn_fb2, L1_xattn_Wq, L1_xattn_bq, L1_xattn_Wk, L1_xattn_bk, L1_xattn_Wv, L1_xattn_bv, L1_xattn_Wo, L1_xattn_bo, L1_ffn_Wr, L1_ffn_br, L1_ffn_W_up, L1_ffn_b_up, L1_ffn_W_down, L1_ffn_b_down):
    import jax
    import jax.numpy as jnp

    def _L0_xattn_ref(q, k, v, Wq, bq, Wk, bk, Wv, bv, Wff, bff):
        import math
        import jax, jax.numpy as jnp
        import numpy as np
        EMB_DIM = 256
        CFG_N_HEADS = 16
        N_HEADS = CFG_N_HEADS if CFG_N_HEADS >= EMB_DIM else 1
        B, T, C = q.shape
        H = N_HEADS
        D = C // H
        qp = (q @ Wq.T + bq).reshape(B, T, H, D).transpose(0, 2, 1, 3)
        kp = (k @ Wk.T + bk).reshape(B, T, H, D).transpose(0, 2, 1, 3)
        vp = (v @ Wv.T + bv).reshape(B, T, H, D).transpose(0, 2, 1, 3)
        scale = 1.0 / math.sqrt(D)
        scores = jnp.einsum('bhqd,bhkd->bhqk', qp, kp) * scale
        causal = jnp.tril(jnp.ones((T, T), dtype=bool))
        scores = jnp.where(causal[None, None, :, :], scores, -jnp.inf)
        attn = jax.nn.softmax(scores, axis=-1)
        out = jnp.einsum('bhqk,bhkd->bhqd', attn, vp)
        out = out.transpose(0, 2, 1, 3).reshape(B, T, C)
        return out @ Wff.T + bff

    def _L0_ffn_ref(x, Wr, W1, b1, W2, b2, fw1, fb1, fw2, fb2):
        import jax, jax.numpy as jnp
        import numpy as np
        E = 8
        TOP_K = 2
        CAP_FACTOR = 1.25
        MIN_CAP = 4
        SCORE_SCALE = 1.0

        def _ffn(x, w1, b1, w2, b2):
            return jax.nn.gelu(x @ w1 + b1, approximate=False) @ w2 + b2
        B, S, D = x.shape
        T = B * S
        x_flat = x.reshape(T, D)
        logits = x_flat @ Wr.T * SCORE_SCALE
        probs = jax.nn.softmax(logits, axis=-1)
        topk_scores, topk_experts = jax.lax.top_k(probs, TOP_K)
        topk_scores = topk_scores / jnp.clip(topk_scores.sum(-1, keepdims=True), 1e-09, None)
        cap = max(int(CAP_FACTOR * (T * TOP_K / E)), MIN_CAP)
        y_fb = _ffn(x_flat, fw1, fb1, fw2, fb2)
        y_flat = jnp.zeros_like(x_flat)
        fallback = jnp.zeros((T,), bool)
        tok_ids = jnp.arange(T, dtype=jnp.int32)
        for e in range(E):
            match = topk_experts == e
            elig = match.any(-1) & ~fallback
            pos = jnp.cumsum(elig) - 1
            kept = elig & (pos < cap)
            overflow = elig & (pos >= cap)
            slot = jnp.where(kept, pos, cap)
            buf = jnp.zeros((cap + 1,), jnp.int32).at[slot].set(tok_ids)
            vmask = jnp.zeros((cap + 1,), bool).at[slot].set(kept)
            idx = buf[:cap]
            valid = vmask[:cap]
            x_e = x_flat[idx]
            y_e = _ffn(x_e, W1[e], b1[e], W2[e], b2[e])
            w_tok = (topk_scores * match).sum(-1)
            w = jnp.where(valid, w_tok[idx], 0.0)
            y_flat = y_flat.at[idx].add(y_e * w[:, None])
            y_flat = jnp.where(overflow[:, None], y_fb, y_flat)
            fallback = fallback | overflow
        return y_flat.reshape(B, S, D)

    def _L1_xattn_ref(query, key, value, Wq, bq, Wk, bk, Wv, bv, Wo, bo):
        import jax, jax.numpy as jnp
        import numpy as np
        EMBED_DIM = 256
        NUM_HEADS = 16
        HEAD_DIM = EMBED_DIM // NUM_HEADS
        SEG_LENS = [256, 512, 1024]
        DIL_RATIOS = [1, 2, 4]
        NEG = -100000000.0

        def _branch(q, k, v, sl, dr, L):
            B = q.shape[0]
            H, D = (NUM_HEADS, HEAD_DIM)
            sl = min(sl, L)
            pad = -L % sl
            if pad:
                pw = ((0, 0), (0, pad), (0, 0), (0, 0))
                q, k, v = (jnp.pad(q, pw), jnp.pad(k, pw), jnp.pad(v, pw))
            n = (L + pad) // sl
            qs = q.reshape(B * n, sl, H, D)
            ks = k.reshape(B * n, sl, H, D)
            vs = v.reshape(B * n, sl, H, D)
            hg = H // dr
            g = sl // dr
            grp = jnp.arange(H) // hg
            pos = jnp.arange(g)[:, None] * dr + grp[None]
            hidx = jnp.arange(H)[None, :]
            sp = lambda x: x[:, pos, hidx, :]
            qd, kd, vd = (sp(qs), sp(ks), sp(vs))
            scores = jnp.einsum('bqhd,bkhd->bhqk', qd, kd) * D ** (-0.5)
            mask = jnp.tril(jnp.ones((g, g), bool))
            scores = jnp.where(mask, scores, -jnp.inf)
            lse = jax.nn.logsumexp(scores, axis=-1)
            o = jnp.einsum('bhqk,bkhd->bqhd', jnp.exp(scores - lse[..., None]), vd)
            hcol = jnp.arange(H)[:, None]
            od = jnp.zeros((B * n, H, sl, D), o.dtype).at[:, hcol, pos.T].set(o.transpose(0, 2, 1, 3))
            ld = jnp.zeros((B * n, H, sl), lse.dtype).at[:, hcol, pos.T].set(lse)
            ld = jnp.where(ld == 0.0, NEG, ld)
            od = od.reshape(B, n, H, sl, D).transpose(0, 2, 1, 3, 4)
            od = od.reshape(B, H, n * sl, D)[:, :, :L]
            ld = ld.reshape(B, n, H, sl).transpose(0, 2, 1, 3).reshape(B, H, n * sl)[:, :, :L]
            return (od, ld)
        B, L, E = query.shape
        H, D = (NUM_HEADS, HEAD_DIM)
        q = (query @ Wq.T + bq).reshape(B, L, H, D)
        k = (key @ Wk.T + bk).reshape(B, L, H, D)
        v = (value @ Wv.T + bv).reshape(B, L, H, D)
        outs, lses = ([], [])
        for sl, dr in zip(SEG_LENS, DIL_RATIOS):
            o, l = _branch(q, k, v, sl, dr, L)
            outs.append(o)
            lses.append(l)
        lse_all = jnp.stack(lses, 0)[..., None]
        m = lse_all.max(0)
        w = jnp.exp(lse_all - m)
        w = w / w.sum(0)
        w = jax.lax.stop_gradient(w)
        out = sum((o * wi.astype(o.dtype) for o, wi in zip(outs, w)))
        out = out.transpose(0, 2, 1, 3).reshape(B, L, E)
        return out @ Wo.T + bo

    def _L1_ffn_ref(x, Wr, br, W_up, b_up, W_down, b_down):
        import jax, jax.numpy as jnp
        import numpy as np
        B, S, H = (4, 512, 256)
        E = 8
        GS = 2
        NG = E // GS
        F = int(H * 4 * (2.0 / 3.0))
        b, s, h = x.shape
        n_tok = b * s
        k = n_tok // E
        xf = x.reshape(n_tok, h)
        logits = xf @ Wr + br
        Sm = jax.nn.softmax(logits, axis=-1)
        G_t, idx_t = jax.lax.top_k(Sm.T, k)
        G = G_t.T
        idx = idx_t.T
        tokens = xf[idx]
        group = jnp.arange(E) // GS
        Wu = W_up[group]
        bu = b_up[group]
        mid = jax.nn.silu(jnp.einsum('keh,ehf->kef', tokens, Wu) + bu)
        out = jnp.einsum('kef,efh->keh', mid, W_down) + b_down
        y = jnp.zeros_like(xf).at[idx].add(G[..., None] * out)
        return y.reshape(b, s, h)
    x = x + jnp.tanh(g_xattn[0]) * _L0_xattn_ref(_layernorm(x, axis=-1), ctx_1024, ctx_1024, L0_xattn_Wq, L0_xattn_bq, L0_xattn_Wk, L0_xattn_bk, L0_xattn_Wv, L0_xattn_bv, L0_xattn_Wff, L0_xattn_bff)
    x = x + jnp.tanh(g_ffn[0]) * _L0_ffn_ref(_layernorm(x, axis=-1), L0_ffn_Wr, L0_ffn_W1, L0_ffn_b1, L0_ffn_W2, L0_ffn_b2, L0_ffn_fw1, L0_ffn_fb1, L0_ffn_fw2, L0_ffn_fb2)
    x = x + jnp.tanh(g_xattn[1]) * _L1_xattn_ref(_layernorm(x, axis=-1), ctx_1024, ctx_1024, L1_xattn_Wq, L1_xattn_bq, L1_xattn_Wk, L1_xattn_bk, L1_xattn_Wv, L1_xattn_bv, L1_xattn_Wo, L1_xattn_bo)
    x = x + jnp.tanh(g_ffn[1]) * _L1_ffn_ref(_layernorm(x, axis=-1), L1_ffn_Wr, L1_ffn_br, L1_ffn_W_up, L1_ffn_b_up, L1_ffn_W_down, L1_ffn_b_down)
    return x

_drawn_inputs = setup_inputs


def setup_inputs(seed=0):
    import zlib

    import numpy as np

    out = dict(_drawn_inputs(seed))
    spreads = {'g_ffn': (-1.0, 0.6),
     'L0_ffn_b1': (0.0, 0.307),
     'L0_ffn_b2': (0.0, 0.1),
     'L0_ffn_fb1': (0.0, 0.1),
     'L0_ffn_fb2': (0.0, 0.1),
     'L1_xattn_bq': (0.0, 0.8),
     'L1_xattn_bk': (0.0, 2.0),
     'L1_xattn_bv': (0.0, 0.286),
     'L1_xattn_bo': (0.0, 0.1),
     'L1_ffn_br': (0.0, 0.338)}
    factors = {'L0_xattn_bq': 3.711,
     'L0_xattn_bk': 64.0,
     'L1_xattn_Wq': 8.0,
     'L1_xattn_Wk': 8.0,
     'L1_ffn_b_up': 29.39,
     'L1_ffn_b_down': 8.0}
    for name, (base, spread) in spreads.items():
        noise = np.random.default_rng([zlib.crc32(name.encode()), seed]).standard_normal(out[name].shape)
        drawn = base * np.exp(spread * noise) if base else spread * noise
        out[name] = jnp.asarray(drawn.astype(out[name].dtype))
    for name, factor in factors.items():
        out[name] = (out[name] * factor).astype(out[name].dtype)
    return out
```

```python
from contextlib import ExitStack

import concourse.bass as bass
from concourse import mybir

F32 = mybir.dt.float32
F16 = mybir.dt.float16
I32 = mybir.dt.int32
U32 = mybir.dt.uint32
ALU = mybir.AluOpType
ACT = mybir.ActivationFunctionType
AX_X = mybir.AxisListType.X

P = 128
NEG = -1.0e30
EPS = 1.0e-5


class Shapes:

    def __init__(self, ins):
        self.B, self.T, self.D = ins["x"].shape
        self.N = self.B * self.T
        self.C = self.D // P
        self.TPB = self.T // P
        self.NT = self.N // P
        self.E = ins["L0_ffn_W1"].shape[0]
        self.F0 = ins["L0_ffn_W1"].shape[2]
        self.CAP = max(int(1.25 * (self.N * 2 / self.E)), 4)
        self.CT = self.CAP // P
        self.ROW = self.D + self.E
        self.H = 16
        self.HD = self.D // self.H
        self.F1 = ins["L1_ffn_W_up"].shape[2]
        self.K1 = self.N // self.E
        self.KT = self.K1 // P
        assert self.CAP % P == 0 and self.T % P == 0 and self.D % P == 0 and self.K1 % P == 0


def col(vec):
    return vec.rearrange("(c p) -> p c", p=P)


def row(vec):
    return vec.partition_broadcast(P)


def chunks(mat):
    return mat.rearrange("(c p) n -> p c n", p=P)


def apart(eng, passed):
    eng.sem_inc(passed, 1)


def stage_semaphores(nc, ctx, prefix):
    taken = []

    def release():
        nc.clear_and_free_semaphores(taken)
        nc.all_engine_barrier()

    ctx.callback(release)

    def sem(name):
        taken.append(nc.alloc_semaphore(prefix + name))
        return taken[-1]
    return sem


def attention_causal(nc, S, ins, dram, keep):
    B, T, D, C, E = S.B, S.T, S.D, S.C, S.E
    QK = P + T
    assert S.TPB == 2 and C == 2
    INV = float(D) ** -0.5
    ident, ones, tg, wT_out, match = (keep[n] for n in ("ident", "ones", "tg", "wT_out", "match"))
    with ExitStack() as ctx:
        def sb(name, shape, dt=F32):
            return ctx.enter_context(nc.sbuf_tensor("a_" + name, shape, dt))

        def pb(name, shape):
            return ctx.enter_context(nc.psum_tensor("a_" + name, shape, F32))

        sem = stage_semaphores(nc, ctx, "a_")
        s_pass = sem("pass"); s_passd = sem("passd"); s_passs = sem("passs")

        names = ["L0_xattn_Wq", "L0_xattn_Wk", "L0_xattn_Wv", "L0_xattn_Wff",
                 "L1_xattn_Wk", "L1_xattn_Wv", "L1_xattn_Wq", "L1_xattn_Wo"]
        w = {n: sb(n, [P, C, D]) for n in names}
        wr0 = sb("wr0", [E, D])
        cols = {n: sb(n, [P, C]) for n in ("L0_xattn_bq", "L0_xattn_bk", "L0_xattn_bv", "L1_xattn_bk")}
        bff = sb("bff", [P, D])
        bv1 = sb("bv1", [P, D])
        gates = sb("gates", [P, 4])
        mask = sb("mask", [P, QK])
        expert_no = sb("expert_no", [P, E])
        half = sb("half", [P, 2])
        mqk = sb("mqk", [P, C, D])
        bprime = sb("bprime", [P, C])
        ucol = sb("ucol", [P, C])
        c0 = sb("c0", [P, 1])
        bqbk = sb("bqbk", [P, C])
        bvb = sb("bvb", [P, C, P])
        wffT = sb("wffT", [P, C, D])
        wvf = sb("wvf", [P, C, D])
        brow = sb("brow", [P, D])
        wkT1 = sb("wkT1", [P, C, D])
        wvT1 = sb("wvT1", [P, C, D])
        wr0T = sb("wr0T", [P, C, E])

        x_in = [sb(f"x_in{u}", [P, 2, D]) for u in range(2)]
        c_in = [sb(f"c_in{u}", [P, 2, D]) for u in range(2)]
        st = [sb(f"st{u}", [P, 2, 6]) for u in range(2)]
        mv = [sb(f"mv{u}", [P, 2, 2]) for u in range(2)]
        var = [sb(f"var{u}", [P, 2]) for u in range(2)]
        rstd = [sb(f"rstd{u}", [P, 2]) for u in range(2)]
        nmr = [sb(f"nmr{u}", [P, 2]) for u in range(2)]
        xn = [sb(f"xn{u}", [P, 2, D]) for u in range(2)]
        xb = [sb(f"xb{u}", [P, 2, D]) for u in range(2)]
        xT = [sb(f"xT{u}", [P, C, T]) for u in range(2)]
        cT = [sb(f"cT{u}", [P, C, T]) for u in range(2)]
        qT = [sb(f"qT{u}", [P, C, T]) for u in range(2)]
        kT = [sb(f"kT{u}", [P, C, T]) for u in range(2)]
        kh = [sb(f"kh{u}", [P, C, T], F16) for u in range(2)]
        kl = [sb(f"kl{u}", [P, C, T], F16) for u in range(2)]
        v1 = [sb(f"v1{u}", [P, 2, D]) for u in range(2)]
        vp = [sb(f"vp{u}", [P, 2, D]) for u in range(2)]
        rr = [sb(f"rr{u}", [P, 2]) for u in range(2)]
        sc = [sb(f"sc{u}", [P, QK]) for u in range(2)]
        mx = [sb(f"mx{u}", [P, 2]) for u in range(2)]
        nm = [sb(f"nm{u}", [P, 2]) for u in range(2)]
        z = [sb(f"z{u}", [P, 2]) for u in range(2)]
        rz = [sb(f"rz{u}", [P, 2]) for u in range(2)]
        zt = [sb(f"zt{u}", [P, 2]) for u in range(2)]
        pr = [sb(f"pr{u}", [P, QK]) for u in range(2)]
        prT = [sb(f"prT{u}", [P, QK]) for u in range(2)]
        x1 = [sb(f"x1{u}", [P, 2, D]) for u in range(2)]
        st1 = [sb(f"st1{u}", [P, 2, 6]) for u in range(2)]
        mv1 = [sb(f"mv1{u}", [P, 2, 2]) for u in range(2)]
        var1 = [sb(f"var1{u}", [P, 2]) for u in range(2)]
        rstd1 = [sb(f"rstd1{u}", [P, 2]) for u in range(2)]
        nmr1 = [sb(f"nmr1{u}", [P, 2]) for u in range(2)]
        rows = [sb(f"rows{u}", [P, 2, S.ROW]) for u in range(2)]
        x1T = [sb(f"x1T{u}", [P, C, T]) for u in range(2)]
        lg = [sb(f"lg{u}", [P, 2, E]) for u in range(2)]
        top = [sb(f"top{u}", [P, 2, 8]) for u in range(2)]
        tix = [sb(f"tix{u}", [P, 2, 8], U32) for u in range(2)]
        tixf = [sb(f"tixf{u}", [P, 2, 2]) for u in range(2)]
        dl = [sb(f"dl{u}", [P, 2]) for u in range(2)]
        el = [sb(f"el{u}", [P, 2]) for u in range(2)]
        el1 = [sb(f"el1{u}", [P, 2]) for u in range(2)]
        p1 = [sb(f"p1{u}", [P, 2]) for u in range(2)]
        pg = [sb(f"pg{u}", [P, 2, 2]) for u in range(2)]
        oh = [sb(f"oh{u}", [P, 2, 2, E]) for u in range(2)]
        og = [sb(f"og{u}", [P, 2, 2, E]) for u in range(2)]

        ps_x, ps_c, ps_q, ps_k, ps_v, ps_w, ps_s, ps_p = (
            pb(n, [P, 512]) for n in ("ps_x", "ps_c", "ps_q", "ps_k", "ps_v", "ps_w", "ps_s", "ps_p"))
        LG = QK + 2

        s_ldw = sem("ldw"); s_ldb = sem("ldb"); s_ldx = [sem("ldx0"), sem("ldx1")]; s_ldc = [sem("ldc0"), sem("ldc1")]
        s_cst = sem("cst"); s_tg = sem("tg"); s_set = sem("set"); s_fold = sem("fold"); s_sev = sem("sev")
        s_brow = sem("brow")
        s_st = sem("st"); s_mv = sem("mv"); s_var = sem("var"); s_small = sem("small"); s_wffT = sem("wffT")
        s_wout = sem("wout"); s_wr0 = sem("wr0"); s_wvf = sem("wvf"); s_zst = sem("zst"); s_rstd = sem("rstd")
        s_mr = sem("mr")
        s_nmr = sem("nmr"); s_xn = sem("xn")
        s_xb = sem("xb"); s_ptx = sem("ptx"); s_ptc = sem("ptc"); s_xT = sem("xT"); s_cT = sem("cT")
        s_pq = sem("pq"); s_qT = sem("qT"); s_pk = sem("pk"); s_kT = sem("kT"); s_kh = sem("kh")
        s_kl = sem("kl"); s_kst = [sem("kst0"), sem("kst1")]
        s_pv = sem("pv"); s_v = sem("v"); s_vst = [sem("vst0"), sem("vst1")]; s_pvp = sem("pvp"); s_vp = sem("vp")
        s_ps = sem("ps"); s_rr = sem("rr"); s_sc = sem("sc"); s_mx = sem("mx"); s_nm = sem("nm")
        s_pr = sem("pr"); s_ppt = sem("ppt"); s_prT = sem("prT"); s_po = sem("po")
        s_rz = sem("rz"); s_zt = sem("zt"); s_x1 = sem("x1"); s_xst = [sem("xst0"), sem("xst1")]
        s_st1 = sem("st1"); s_mv1 = sem("mv1"); s_rstd1 = sem("rstd1"); s_var1 = sem("var1")
        s_mr1 = sem("mr1"); s_nmr1 = sem("nmr1")
        s_xn1 = sem("xn1"); s_px1 = sem("px1"); s_x1T = sem("x1T"); s_plg = sem("plg")
        s_lg = sem("lg"); s_top = sem("top"); s_tix = sem("tix"); s_tixf = sem("tixf"); s_dl = sem("dl")
        s_el = sem("el"); s_el1 = sem("el1"); s_p1 = sem("p1"); s_pg = sem("pg")
        s_oh = sem("oh"); s_og = sem("og"); s_gate = sem("gate"); s_rst = [sem("rst0"), sem("rst1")]

        def pipeline(step):
            def run(eng):
                step(0, 0, True, False, False)
                step(1, 1, True, True, False)
                with eng.Fori(0, B // 2 - 2) as i:
                    step(i * 2 + 2, 0, True, True, True)
                    step(i * 2 + 3, 1, True, True, True)
                step(B - 2, 0, True, True, True)
                step(B - 1, 1, True, True, True)
                step(B, 0, False, True, True)
                step(B + 1, 1, False, False, True)
            return run

        def after(eng, what, n, back=0, per=1):
            if not isinstance(n, int) or n >= back:
                eng.wait_ge(what, (n - back) * per + per)

        def landed(eng, pair, n, u, back=0, per=16):
            if not isinstance(n, int) or n >= back:
                par = (u + back) % 2
                eng.wait_ge(pair[par], (n - back - par) * (per // 2) + per)

        def has_next(n):
            return not isinstance(n, int) or n + 1 < B

        def halves(bank):
            return bank[:].rearrange("p (c t) -> p c t", c=2)

        block = ctx.enter_context(nc.Block())
        x_t = ins["x"].rearrange("b (j p) d -> b p j d", p=P)
        c_t = ins["ctx_1024"].rearrange("b (j p) d -> b p j d", p=P)
        res_t = dram["res"][0:S.N, :].rearrange("(b j p) d -> b p j d", b=B, p=P)
        rows_t = dram["rows"].rearrange("(b j p) d -> b p j d", b=B, p=P)

        @block.sync
        def _(sp):
            def load(n, u):
                sp.dma_start(x_in[u][:], x_t[n]).then_inc(s_ldx[u], 16)
                sp.dma_start(c_in[u][:], c_t[n]).then_inc(s_ldc[u], 16)

            load(0, 0)
            for n in names:
                sp.dma_start(w[n][:], chunks(ins[n])).then_inc(s_ldw, 16)
            sp.dma_start(wr0[:], ins["L0_ffn_Wr"]).then_inc(s_ldw, 16)

            def step(n, u, front, back, gate):
                if front and has_next(n):
                    after(sp, s_xn, n, 1, 2)
                    apart(sp, s_passs)
                    after(sp, s_xb, n, 1)
                    after(sp, s_ptc, n, 1)
                    load(n + 1, 1 - u)
                if front:
                    after(sp, s_kl, n)
                    for part, k in enumerate((kh, kl)):
                        sp.dma_start(dram["kT"][n, part].rearrange("(c p) t -> p c t", p=P), k[u][:])\
                            .then_inc(s_kst[u], 16)
                    after(sp, s_v, n)
                    sp.dma_start(dram["v"][n], v1[u][:]).then_inc(s_vst[u], 16)
                if back:
                    after(sp, s_x1, n, 1, 2)
                    sp.dma_start(res_t[n - 1], x1[1 - u][:]).then_inc(s_xst[1 - u], 16)
                if gate:
                    after(sp, s_xn1, n, 2, 2)
                    after(sp, s_gate, n, 2, 2)
                    sp.dma_start(rows_t[n - 2], rows[u][:]).then_inc(s_rst[u], 16)

            pipeline(step)(sp)
            for u in range(2):
                for pair, per in ((s_kst, 32), (s_vst, 16), (s_xst, 16), (s_rst, 16)):
                    sp.wait_ge(pair[u], per * B // 2)

        @block.gpsimd
        def _(pool):
            pool.memset(ident[:], 0.0).then_inc(s_cst, 1)
            pool.memset(ones[:], 1.0).then_inc(s_cst, 1)
            pool.memset(mask[:], 0.0).then_inc(s_cst, 1)
            pool.memset(half[:], -0.5).then_inc(s_cst, 1)
            pool.memset(keep["zeros"][:], 0.0).then_inc(s_cst, 1)
            pool.iota(expert_no[:], pattern=[[1, E]], base=0, channel_multiplier=0,
                      allow_small_or_imprecise_dtypes=True).then_inc(s_cst, 1)
            pool.wait_ge(s_cst, 6)
            pool.affine_select(out=ident[:], in_=ident[:], compare_op=ALU.not_equal, fill=1.0, base=0,
                               pattern=[[-1, P]], channel_multiplier=1).then_inc(s_cst, 1)
            for o in (0, T):
                pool.affine_select(out=mask[:, o:o + P], in_=mask[:, o:o + P], compare_op=ALU.is_ge, fill=NEG,
                                   base=0, pattern=[[-1, P]], channel_multiplier=1).then_inc(s_cst, 1)
            pool.dma_start(dram["res"][S.N:S.N + S.CAP, :].rearrange("(j p) d -> p j d", p=P),
                           keep["zeros"][:].unsqueeze(1).to_broadcast([P, S.CT, D])).then_inc(s_zst, 16)

            def layernorm_scale(n, s_var, var_, rstd_, s_r, mv_, nmr_, s_m, s_n):
                after(pool, s_var, n)
                pool.tensor_tensor(rstd_[:], var_[:], half[:], ALU.pow).then_inc(s_r, 1)
                after(pool, s_r, n)
                pool.tensor_tensor(nmr_[:], mv_[:, :, 0], rstd_[:], ALU.mult).then_inc(s_m, 1)
                after(pool, s_m, n)
                apart(pool, s_pass)
                pool.tensor_scalar(nmr_[:], nmr_[:], -1.0, None, ALU.mult).then_inc(s_n, 1)

            layernorm_scale(0, s_var, var[0], rstd[0], s_rstd, mv[0], nmr[0], s_mr, s_nmr)
            pool.wait_ge(s_brow, 2)

            def step(n, u, front, back, gate):
                if front:
                    if has_next(n):
                        layernorm_scale(n + 1, s_var, var[1 - u], rstd[1 - u], s_rstd, mv[1 - u], nmr[1 - u],
                                        s_mr, s_nmr)
                    landed(pool, s_ldx, n, u)
                    after(pool, s_x1, n, 2, 2)
                    pool.tensor_tensor(xb[u][:], x_in[u][:], brow[:].unsqueeze(1).to_broadcast([P, 2, D]),
                                       ALU.add).then_inc(s_xb, 1)
                    after(pool, s_kT, n)
                    landed(pool, s_kst, n, u, 2, 32)
                    apart(pool, s_pass)
                    pool.tensor_copy(kh[u][:], kT[u][:]).then_inc(s_kh, 1)
                    after(pool, s_kh, n)
                    pool.tensor_tensor(kl[u][:], kT[u][:], kh[u][:], ALU.subtract).then_inc(s_kl, 1)
                if back:
                    v = 1 - u
                    layernorm_scale(n - 1, s_var1, var1[v], rstd1[v], s_rstd1, mv1[v], nmr1[v], s_mr1, s_nmr1)
                if gate:
                    g = n - 2
                    landed(pool, s_rst, g, u, 2)
                    after(pool, s_pg, g, 0, 2)
                    after(pool, s_oh, g, 0, 2)
                    pool.tensor_tensor(match[:, bass.ds(g * 2, 2), :], oh[u][:, :, 0, :], oh[u][:, :, 1, :], ALU.add)\
                        .then_inc(s_gate, 1)
                    for k in range(2):
                        pool.tensor_tensor(og[u][:, :, k, :], oh[u][:, :, k, :],
                                           pg[u][:, :, k:k + 1].to_broadcast([P, 2, E]), ALU.mult)\
                            .then_inc(s_og, 1)
                    after(pool, s_og, g, 0, 2)
                    pool.tensor_tensor(rows[u][:, :, D:S.ROW], og[u][:, :, 0, :], og[u][:, :, 1, :], ALU.add)\
                        .then_inc(s_gate, 1)

            pipeline(step)(pool)
            pool.wait_ge(s_zst, 16)

        @block.scalar
        def _(act):
            for n in cols:
                act.dma_start(cols[n][:], col(ins[n])).then_inc(s_ldb, 16)
            act.dma_start(bff[:], row(ins["L0_xattn_bff"])).then_inc(s_ldb, 16)
            act.dma_start(bv1[:], row(ins["L1_xattn_bv"])).then_inc(s_ldb, 16)
            act.dma_start(gates[:, 0:2], row(ins["g_xattn"])).then_inc(s_ldb, 16)
            act.dma_start(gates[:, 2:4], row(ins["g_ffn"])).then_inc(s_ldb, 16)
            act.wait_ge(s_ldb, 16 * 8)
            act.activation(tg[:], gates[:], ACT.Tanh).then_inc(s_tg, 1)

            def normalise(n, s_n, rstd_, nmr_, src, dst, s_done):
                after(act, s_n, n)
                for j in range(2):
                    act.activation(dst[:, j, 0:D], src[:, j, :], ACT.Identity, bias=nmr_[:, j:j + 1],
                                   scale=rstd_[:, j:j + 1]).then_inc(s_done, 1)

            normalise(0, s_nmr, rstd[0], nmr[0], x_in[0], xn[0], s_xn)
            act.wait_ge(s_fold, 1)
            act.activation(mqk[:], halves(ps_q), ACT.Copy).then_inc(s_sev, 1)
            act.wait_ge(s_fold, 5)
            act.activation(wkT1[:], halves(ps_v), ACT.Copy).then_inc(s_sev, 1)
            act.activation(wvT1[:], halves(ps_w), ACT.Copy).then_inc(s_sev, 1)
            act.wait_ge(s_small, 3)

            def step(n, u, front, back, gate):
                m, v = n - 1, 1 - u
                if front:
                    after(act, s_ptx, n)
                    after(act, s_ps, n, 2)
                    act.activation(xT[u][:], halves(ps_x), ACT.Copy).then_inc(s_xT, 1)
                    after(act, s_pq, n)
                    for c in range(C):
                        last = act.activation(qT[u][:, c, :], ps_q[:, c * T:(c + 1) * T], ACT.Identity,
                                              bias=bprime[:, c:c + 1])
                    last.then_inc(s_qT, 1)
                    if has_next(n):
                        after(act, s_ptx, n, 1)
                        normalise(n + 1, s_nmr, rstd[v], nmr[v], x_in[v], xn[v], s_xn)
                    after(act, s_pk, n)
                    after(act, s_kl, n, 2)
                    for c in range(C):
                        last = act.activation(kT[u][:, c, :], ps_k[:, c * T:(c + 1) * T], ACT.Identity,
                                              bias=cols["L1_xattn_bk"][:, c:c + 1])
                    last.then_inc(s_kT, 1)
                    after(act, s_pvp, n)
                    after(act, s_po, n, 2)
                    act.activation(vp[u][:], halves(ps_w), ACT.Copy).then_inc(s_vp, 1)
                if back:
                    landed(act, s_rst, m, v, 2)
                    after(act, s_x1, m, 0, 2)
                    normalise(m, s_nmr1, rstd1[v], nmr1[v], x1[v], rows[v], s_xn1)
                if front:
                    after(act, s_nm, n, 0, 2)
                    after(act, s_ppt, n, 2)
                    after(act, s_rz, n, 2)
                    act.activation(pr[u][:, 0:P], sc[u][:, 0:P], ACT.Exp, bias=nm[u][:, 0:1], scale=INV,
                                   accum_out=z[u][:, 0:1]).then_inc(s_pr, 1)
                    act.activation(pr[u][:, P:QK], sc[u][:, P:QK], ACT.Exp, bias=nm[u][:, 1:2], scale=INV,
                                   accum_out=z[u][:, 1:2]).then_inc(s_pr, 1)
                if back:
                    after(act, s_px1, m)
                    after(act, s_plg, m, 2)
                    act.activation(x1T[v][:], halves(ps_x), ACT.Copy).then_inc(s_x1T, 1)
                if gate:
                    after(act, s_dl, n, 2)
                    act.activation(el[u][:], dl[u][:], ACT.Exp).then_inc(s_el, 1)

            pipeline(step)(act)

        @block.vector
        def _(dve):
            def stats(n, src, st_, s_st_, mv_, s_mv_, var_, s_var_):
                for j in range(2):
                    dve.bn_stats(st_[:, j, :], src[:, j, :]).then_inc(s_st_, 1)
                after(dve, s_st_, n, 0, 2)
                apart(dve, s_passd)
                for j in range(2):
                    dve.bn_aggr(mv_[:, j, :], st_[:, j, :]).then_inc(s_mv_, 1)
                after(dve, s_mv_, n, 0, 2)
                dve.tensor_scalar(var_[:], mv_[:, :, 1], EPS, None, ALU.add).then_inc(s_var_, 1)

            dve.wait_ge(s_cst, 9)
            dve.wait_ge(s_ldx[0], 16)
            stats(0, x_in[0], st[0], s_st, mv[0], s_mv, var[0], s_var)
            dve.wait_ge(s_ldb, 16 * 8)
            dve.tensor_tensor(bqbk[:], cols["L0_xattn_bq"][:], cols["L0_xattn_bk"][:], ALU.mult).then_inc(s_set, 1)
            dve.tensor_copy(bvb[:], cols["L0_xattn_bv"][:].unsqueeze(2).to_broadcast([P, C, P])).then_inc(s_set, 1)
            dve.wait_ge(s_fold, 2)
            dve.tensor_copy(bprime[:], ps_s[:, 0:2]).then_inc(s_small, 1)
            dve.tensor_copy(ucol[:], ps_s[:, 2:4]).then_inc(s_small, 1)
            dve.tensor_copy(c0[:], ps_s[:, 4:5]).then_inc(s_small, 1)
            dve.wait_ge(s_fold, 3)
            dve.tensor_copy(wffT[:], halves(ps_p)).then_inc(s_wffT, 1)
            dve.wait_ge(s_fold, 7)
            dve.tensor_copy(wT_out[:, 0, :, :], halves(ps_x)).then_inc(s_wout, 1)
            dve.tensor_copy(wT_out[:, 1, :, :], halves(ps_c)).then_inc(s_wout, 1)
            dve.wait_ge(s_fold, 8)
            dve.tensor_copy(wr0T[:], ps_k[:, 0:C * E].rearrange("p (c e) -> p c e", c=C)).then_inc(s_wr0, 1)
            dve.wait_ge(s_fold, 9)
            dve.tensor_copy(wvf[:], halves(ps_q)).then_inc(s_wvf, 1)
            dve.wait_ge(s_fold, 10)
            dve.tensor_tensor(brow[:], ps_p[:, 0:D], bff[:], ALU.add).then_inc(s_brow, 1)
            dve.wait_ge(s_brow, 1)
            dve.wait_ge(s_tg, 1)
            dve.tensor_scalar(brow[:], brow[:], tg[:, 0:1], None, ALU.mult).then_inc(s_brow, 1)

            def step(n, u, front, back, gate):
                m, v = n - 1, 1 - u
                if front:
                    after(dve, s_ptc, n)
                    after(dve, s_ps, n, 2)
                    dve.tensor_copy(cT[u][:], halves(ps_c)).then_inc(s_cT, 1)
                    if has_next(n):
                        landed(dve, s_ldx, n + 1, v)
                        after(dve, s_nmr, n, 1)
                        stats(n + 1, x_in[v], st[v], s_st, mv[v], s_mv, var[v], s_var)
                if back:
                    after(dve, s_ppt, m)
                    after(dve, s_po, m, 2)
                    dve.tensor_copy(prT[v][:], ps_p[:, 0:QK]).then_inc(s_prT, 1)
                    after(dve, s_pr, m, 0, 2)
                    dve.reciprocal(rz[v][:], z[v][:]).then_inc(s_rz, 1)
                    after(dve, s_rz, m)
                    dve.tensor_scalar(zt[v][:], rz[v][:], tg[:, 0:1], None, ALU.mult).then_inc(s_zt, 1)
                if front:
                    after(dve, s_pv, n)
                    landed(dve, s_vst, n, u, 2)
                    dve.tensor_tensor(v1[u][:], halves(ps_v), bv1[:].unsqueeze(1).to_broadcast([P, 2, D]),
                                      ALU.add).then_inc(s_v, 1)
                if back:
                    after(dve, s_po, m)
                    after(dve, s_zt, m)
                    after(dve, s_xb, m)
                    landed(dve, s_xst, m, v, 2)
                    after(dve, s_xn1, m, 2, 2)
                    for j in range(2):
                        dve.scalar_tensor_tensor(out=x1[v][:, j, :], in0=ps_c[:, j * D:(j + 1) * D],
                                                 scalar=zt[v][:, j:j + 1], in1=xb[v][:, j, :],
                                                 op0=ALU.mult, op1=ALU.add).then_inc(s_x1, 1)
                    after(dve, s_x1, m, 0, 2)
                    after(dve, s_nmr1, m, 2)
                    stats(m, x1[v], st1[v], s_st1, mv1[v], s_mv1, var1[v], s_var1)
                if front:
                    after(dve, s_ps, n)
                    dve.tensor_scalar(rr[u][:], ps_s[:, QK:QK + 2], c0[:, 0:1], None, ALU.add).then_inc(s_rr, 1)
                    after(dve, s_rr, n)
                    after(dve, s_pr, n, 2, 2)
                    for j, (a, b) in enumerate(((0, P), (P, QK))):
                        dve.scalar_tensor_tensor(out=sc[u][:, a:b], in0=ps_s[:, a:b], scalar=rr[u][:, j:j + 1],
                                                 in1=mask[:, a:b] if j == 0 else mask2, op0=ALU.add,
                                                 op1=ALU.add).then_inc(s_sc, 1)
                    after(dve, s_sc, n, 0, 2)
                    for j, (a, b) in enumerate(((0, P), (P, QK))):
                        dve.tensor_reduce(mx[u][:, j:j + 1], sc[u][:, a:b], AX_X, ALU.max).then_inc(s_mx, 1)
                    after(dve, s_mx, n, 0, 2)
                    dve.tensor_scalar(nm[u][:], mx[u][:], -INV, None, ALU.mult).then_inc(s_nm, 2)
                if gate:
                    g = n - 2
                    after(dve, s_plg, g)
                    dve.tensor_copy(lg[u][:], ps_s[:, LG:LG + 2 * E].rearrange("p (j e) -> p j e", j=2))\
                        .then_inc(s_lg, 1)
                    after(dve, s_lg, g)
                    apart(dve, s_passd)
                    for j in range(2):
                        dve.max(top[u][:, j, :], lg[u][:, j, :]).then_inc(s_top, 1)
                    after(dve, s_top, g, 0, 2)
                    dve.tensor_tensor(dl[u][:], top[u][:, :, 1], top[u][:, :, 0], ALU.subtract).then_inc(s_dl, 1)
                    for j in range(2):
                        dve.max_index(tix[u][:, j, :], top[u][:, j, :], lg[u][:, j, :]).then_inc(s_tix, 1)
                    after(dve, s_tix, g, 0, 2)
                    after(dve, s_gate, g, 1, 2)
                    dve.tensor_copy(tixf[u][:], tix[u][:, :, 0:2]).then_inc(s_tixf, 1)
                    after(dve, s_tixf, g)
                    for k in range(2):
                        dve.tensor_tensor(oh[u][:, :, k, :], expert_no[:].unsqueeze(1).to_broadcast([P, 2, E]),
                                          tixf[u][:, :, k:k + 1].to_broadcast([P, 2, E]), ALU.is_equal)\
                            .then_inc(s_oh, 1)
                    after(dve, s_el, g)
                    dve.tensor_scalar(el1[u][:], el[u][:], 1.0, None, ALU.add).then_inc(s_el1, 1)
                    after(dve, s_el1, g)
                    dve.reciprocal(p1[u][:], el1[u][:]).then_inc(s_p1, 1)
                    after(dve, s_p1, g)
                    dve.tensor_scalar(pg[u][:, :, 0], p1[u][:], tg[:, 2:3], None, ALU.mult).then_inc(s_pg, 1)
                    dve.scalar_tensor_tensor(out=pg[u][:, :, 1], in0=p1[u][:], scalar=tg[:, 2:3], in1=el[u][:],
                                             op0=ALU.mult, op1=ALU.mult).then_inc(s_pg, 1)

            mask2 = mask[:, P:QK]
            pipeline(step)(dve)

        @block.tensor
        def _(pe):
            def turn(bank, src):
                for r in range(2):
                    for c in range(2):
                        last = pe.transpose(bank[:, c * D + r * P:c * D + (r + 1) * P],
                                            src[:, r, c * P:(c + 1) * P], ident[:])
                return last

            def product(bank, lhs, rhs):
                for r in range(2):
                    for c in range(C):
                        last = pe.matmul(bank[:, r * D:(r + 1) * D], lhs[:, c, r * P:(r + 1) * P], rhs[:, c, :],
                                         start=(c == 0), stop=(c == C - 1))
                return last

            pe.wait_ge(s_cst, 9)
            pe.wait_ge(s_ldw, 16 * (len(names) + 1))
            pe.wait_ge(s_set, 2)
            product(ps_q, w["L0_xattn_Wq"], w["L0_xattn_Wk"]).then_inc(s_fold, 1)
            for j in range(2):
                for c in range(C):
                    pe.matmul(ps_s[:, j:j + 1], w["L0_xattn_Wk"][:, c, j * P:(j + 1) * P],
                              cols["L0_xattn_bq"][:, c:c + 1], start=(c == 0), stop=(c == C - 1))
            for j in range(2):
                for c in range(C):
                    pe.matmul(ps_s[:, 2 + j:3 + j], w["L0_xattn_Wq"][:, c, j * P:(j + 1) * P],
                              cols["L0_xattn_bk"][:, c:c + 1], start=(c == 0), stop=(c == C - 1))
            for c in range(C):
                last = pe.matmul(ps_s[:, 4:5], ones[:], bqbk[:, c:c + 1], start=(c == 0), stop=(c == C - 1))
            last.then_inc(s_fold, 1)
            turn(ps_p, w["L0_xattn_Wff"]).then_inc(s_fold, 1)
            turn(ps_v, w["L1_xattn_Wk"]).then_inc(s_fold, 1)
            turn(ps_w, w["L1_xattn_Wv"]).then_inc(s_fold, 1)
            turn(ps_x, w["L1_xattn_Wq"]).then_inc(s_fold, 1)
            turn(ps_c, w["L1_xattn_Wo"]).then_inc(s_fold, 1)
            for c in range(C):
                last = pe.transpose(ps_k[:, c * E:(c + 1) * E], wr0[:, c * P:(c + 1) * P], ident[0:E, 0:E])
            last.then_inc(s_fold, 1)
            pe.wait_ge(s_sev, 1)
            pe.wait_ge(s_wffT, 1)
            product(ps_q, w["L0_xattn_Wv"], wffT).then_inc(s_fold, 1)
            for c in range(C):
                last = pe.matmul(ps_p[:, 0:D], bvb[:, c, :], wffT[:, c, :], start=(c == 0), stop=(c == C - 1))
            last.then_inc(s_fold, 1)
            pe.wait_ge(s_wout, 2)
            pe.wait_ge(s_sev, 3)
            pe.wait_ge(s_wr0, 1)
            pe.wait_ge(s_wvf, 1)
            pe.wait_ge(s_brow, 1)
            pe.wait_ge(s_small, 3)

            def step(n, u, front, back, gate):
                m, v = n - 1, 1 - u
                if front:
                    after(pe, s_xn, n, 0, 2)
                    after(pe, s_x1T, n, 2)
                    turn(ps_x, xn[u]).then_inc(s_ptx, 1)
                    landed(pe, s_ldc, n, u)
                    after(pe, s_x1, n, 2, 2)
                    turn(ps_c, c_in[u]).then_inc(s_ptc, 1)
                    after(pe, s_xT, n)
                    after(pe, s_qT, n, 1)
                    product(ps_q, mqk, xT[u]).then_inc(s_pq, 1)
                if back:
                    after(pe, s_pr, m, 0, 2)
                    after(pe, s_prT, m, 1)
                    for a in range(0, QK, P):
                        last = pe.transpose(ps_p[:, a:a + P], pr[v][:, a:a + P], ident[:])
                    last.then_inc(s_ppt, 1)
                if front:
                    after(pe, s_cT, n)
                    after(pe, s_kT, n, 1)
                    product(ps_k, wkT1, cT[u]).then_inc(s_pk, 1)
                    after(pe, s_v, n, 1)
                    product(ps_v, cT[u], wvT1).then_inc(s_pv, 1)
                    after(pe, s_vp, n, 1)
                    product(ps_w, cT[u], wvf).then_inc(s_pvp, 1)
                if back:
                    after(pe, s_prT, m)
                    after(pe, s_vp, m)
                    if front:
                        after(pe, s_cT, n)
                    pe.matmul(ps_c[:, 0:D], prT[v][:, 0:P], vp[v][:, 0, :], start=True, stop=True)
                    pe.matmul(ps_c[:, D:2 * D], prT[v][:, P:2 * P], vp[v][:, 0, :], start=True, stop=False)
                    pe.matmul(ps_c[:, D:2 * D], prT[v][:, 2 * P:3 * P], vp[v][:, 1, :], start=False, stop=True)\
                        .then_inc(s_po, 1)
                if front:
                    after(pe, s_qT, n)
                    after(pe, s_sc, n, 1, 2)
                    for a, q, keys in ((0, 0, P), (P, 1, T)):
                        for c in range(C):
                            pe.matmul(ps_s[:, a:a + keys], qT[u][:, c, q * P:(q + 1) * P], cT[u][:, c, 0:keys],
                                      start=(c == 0), stop=(c == C - 1))
                    for q in range(2):
                        for c in range(C):
                            last = pe.matmul(ps_s[:, QK + q:QK + q + 1], xT[u][:, c, q * P:(q + 1) * P],
                                             ucol[:, c:c + 1], start=(c == 0), stop=(c == C - 1))
                    last.then_inc(s_ps, 1)
                if back:
                    after(pe, s_xn1, m, 0, 2)
                    if front:
                        after(pe, s_xT, n)
                    turn(ps_x, rows[v]).then_inc(s_px1, 1)
                    after(pe, s_x1T, m)
                    after(pe, s_lg, m, 1)
                    for j in range(2):
                        for c in range(C):
                            last = pe.matmul(ps_s[:, LG + j * E:LG + (j + 1) * E], x1T[v][:, c, j * P:(j + 1) * P],
                                             wr0T[:, c, :], start=(c == 0), stop=(c == C - 1))
                    last.then_inc(s_plg, 1)

            pipeline(step)(pe)


def experts_capacity(nc, S, ins, dram, keep):
    N, D, C, E, F, NT, CT, CAP = S.N, S.D, S.C, S.E, S.F0, S.NT, S.CT, S.CAP
    FC = F // P
    HALF = CAP // 2
    WS = 256.0
    FIRST = 3
    assert F % P == 0 and HALF <= 512 and FIRST + CT <= FC
    ident, ones, tg, match = keep["ident"], keep["ones"], keep["tg"], keep["match"]
    with ExitStack() as ctx:
        def sb(name, shape, dt=F32):
            return ctx.enter_context(nc.sbuf_tensor("b_" + name, shape, dt))

        def pb(name, shape):
            return ctx.enter_context(nc.psum_tensor("b_" + name, shape, F32))

        sem = stage_semaphores(nc, ctx, "b_")
        s_pass = sem("pass"); s_passd = sem("passd"); s_passs = sem("passs")

        tri = sb("tri", [P, P], F16)
        ones16 = sb("ones16", [P, P], F16)
        lane = sb("lane", [P, P], F16)
        tile_no = sb("tile_no", [P, CT], F16)
        token1 = sb("token1", [P, NT])
        spare1 = sb("spare1", [P, CT])
        one_row = sb("one_row", [P, NT])
        b1_in = sb("b1_in", [E * FC, P])
        b1T = sb("b1T", [P, E * FC])
        b2 = sb("b2", [P, E, D])

        free = sb("free", [P, NT])
        elig = sb("elig", [P, E, NT])
        elig16 = sb("elig16", [P, E, NT], F16)
        cum = sb("cum", [P, NT])
        excl = sb("excl", [P, NT], F16)
        over = sb("over", [P, NT])
        pos = sb("pos", [P, E, NT])
        inside = sb("inside", [P, E, NT])
        value = sb("value", [P, E, NT])
        slot = sb("slot", [P, E, NT], I32)
        slot_lo = sb("slot_lo", [P, E, NT], I32)
        slot_hi = sb("slot_hi", [P, E, NT], I32)
        lo16 = sb("lo16", [P, E, NT], F16)
        hi16 = sb("hi16", [P, E, NT], F16)
        fallen, fallen_n = keep["fallen"], keep["fallen_n"]
        fallen_any = sb("fallen_any", [P, 1])

        at_lo = [sb(f"at_lo{u}", [P, NT, P], F16) for u in range(2)]
        at_hi = [sb(f"at_hi{u}", [P, NT, CT], F16) for u in range(2)]
        vhi = [sb(f"vhi{u}", [P, NT, CT], F16) for u in range(2)]
        who = sb("who", [P, E, CT])
        empty_g = sb("empty_g", [P, CT])
        empty_s = sb("empty_s", [P, CT])
        jump = sb("jump", [P, CT])
        g_idx = [sb(f"g_idx{u}", [P, CT], I32) for u in range(2)]
        s_idx = [sb(f"s_idx{u}", [P, CT], I32) for u in range(2)]
        xg = [sb(f"xg{u}", [P, CT, S.ROW]) for u in range(2)]
        gate = [sb(f"gate{u}", [P, CT]) for u in range(2)]
        b1 = [sb(f"b1{u}", [P, FC]) for u in range(2)]
        xh = [sb(f"xh{u}", [P, C, CAP], F16) for u in range(2)]
        xl = [sb(f"xl{u}", [P, C, CAP], F16) for u in range(2)]
        w1 = sb("w1", [P, C, F])
        w2 = sb("w2", [P, FC, D])
        w1h = [sb(f"w1h{u}", [P, C, F], F16) for u in range(2)]
        w1l = [sb(f"w1l{u}", [P, C, F], F16) for u in range(2)]
        w2h = [sb(f"w2h{u}", [P, FC, D], F16) for u in range(2)]
        w2l = [sb(f"w2l{u}", [P, FC, D], F16) for u in range(2)]
        h = [sb(f"h{k}", [P, 2, HALF]) for k in range(2)]
        hh = sb("hh", [P, FC, CAP], F16)
        hl = sb("hl", [P, FC, CAP], F16)
        yb = sb("yb", [P, CT, D])
        y = sb("y", [P, CT, D])

        ps_h = [pb(f"ps_h{k}", [P, 2, 512]) for k in range(2)]
        ps_y = [pb(f"ps_y{k}", [P, 512]) for k in range(2)]
        ps_x = [ps_y[k][:, 0:C * P].rearrange("p (c t) -> p c t", c=C) for k in range(2)]
        ps_i = pb("ps_i", [P, 512])
        POS, IDX, BT, ANY = 0, E * NT, E * NT + E * CT, E * NT + E * CT + E * FC

        s_cst = sem("cst"); s_ldb = sem("ldb"); s_free = sem("free"); s_elig = sem("elig"); s_e16 = sem("e16")
        s_cum = sem("cum"); s_excl = sem("excl"); s_ppos = sem("ppos"); s_pos = sem("pos"); s_over = sem("over")
        s_in1 = sem("in1"); s_in2 = sem("in2"); s_value = sem("value"); s_slot = sem("slot")
        s_split = sem("split"); s_lohi = sem("lohi"); s_pb1 = sem("pb1"); s_b1T = sem("b1T")
        s_fell = sem("fell"); s_fsum = sem("fsum"); s_pany = sem("pany"); s_any = sem("any")
        s_atlo = sem("atlo"); s_athi = sem("athi"); s_vhi = sem("vhi"); s_pidx = sem("pidx"); s_who = sem("who")
        s_emg = sem("emg"); s_gi = sem("gi"); s_ems = sem("ems"); s_jmp = sem("jmp"); s_si = sem("si")
        s_g = [sem("g0"), sem("g1")]; s_w = sem("w"); s_gate = sem("gate"); s_b1 = sem("b1")
        s_px = sem("px"); s_xh = sem("xh"); s_xl = sem("xl"); s_wh = sem("wh"); s_wl = sem("wl")
        s_ph = sem("ph"); s_h = sem("h"); s_hh = sem("hh"); s_hl = sem("hl")
        s_py = sem("py"); s_yb = sem("yb"); s_y = sem("y"); s_add = sem("add")

        def pipeline(step):
            def run(eng):
                step(-2, 0, True, False, False)
                step(-1, 1, True, True, False)
                with eng.Fori(0, E // 2 - 1) as i:
                    step(i * 2, 0, True, True, True)
                    step(i * 2 + 1, 1, True, True, True)
                step(E - 2, 0, False, True, True)
                step(E - 1, 1, False, False, True)
            return run

        def count(eng, what, value):
            if not isinstance(value, int) or value > 0:
                eng.wait_ge(what, value)

        WP = 4

        def pieces(stage, high, low):
            out = []
            for a, b, c in zip(stage, high, low):
                flat = [t[:].rearrange("p a b -> p (a b)") for t in (a, b, c)]
                n = flat[0].shape[1] // WP
                out += [[f[:, k * n:(k + 1) * n] for f in flat] for k in range(WP)]
            return out

        block = ctx.enter_context(nc.Block())

        @block.sync
        def _(sp):
            sp.dma_start(b1_in[:], ins["L0_ffn_b1"].rearrange("e (c p) -> (e c) p", p=P)).then_inc(s_ldb, 16)
            sp.dma_start(b2[:], ins["L0_ffn_b2"].partition_broadcast(P)).then_inc(s_ldb, 16)

            def load(e):
                sp.dma_start(w1[:], ins["L0_ffn_W1"][e].rearrange("(c p) f -> p c f", p=P)).then_inc(s_w, 16)
                sp.dma_start(w2[:], ins["L0_ffn_W2"][e].rearrange("(c p) d -> p c d", p=P)).then_inc(s_w, 16)

            load(0)

            def step(e, u, slots, rows, products):
                if rows and not (isinstance(e, int) and e + 2 >= E):
                    sp.wait_ge(s_wl, (e + 2) * 2 * WP)
                    load(e + 2)

            pipeline(step)(sp)

        @block.gpsimd
        def _(pool):
            pool.memset(tri[:], 1.0).then_inc(s_cst, 1)
            pool.memset(ones16[:], 1.0).then_inc(s_cst, 1)
            pool.memset(one_row[:], 1.0).then_inc(s_cst, 1)
            pool.iota(lane[:], pattern=[[1, P]], base=0, channel_multiplier=0,
                      allow_small_or_imprecise_dtypes=True).then_inc(s_cst, 1)
            pool.iota(tile_no[:], pattern=[[1, CT]], base=0, channel_multiplier=0,
                      allow_small_or_imprecise_dtypes=True).then_inc(s_cst, 1)
            pool.iota(token1[:], pattern=[[P, NT]], base=1, channel_multiplier=1,
                      allow_small_or_imprecise_dtypes=True).then_inc(s_cst, 1)
            pool.iota(spare1[:], pattern=[[P, CT]], base=N + 1, channel_multiplier=1,
                      allow_small_or_imprecise_dtypes=True).then_inc(s_cst, 1)
            pool.wait_ge(s_cst, 7)
            pool.affine_select(out=tri[:], in_=tri[:], compare_op=ALU.is_ge, fill=0.0, base=0,
                               pattern=[[1, P]], channel_multiplier=-1).then_inc(s_cst, 1)

            def step(e, u, slots, rows, products):
                v = 1 - u
                if rows:
                    pool.wait_ge(s_gi, e + 2)
                    count(pool, s_px, e * CT)
                    count(pool, s_gate, e)
                    apart(pool, s_pass)
                    for j in range(CT):
                        pool.indirect_dma_start(
                            out=xg[v][:, j, :], out_offset=None, in_=dram["rows"],
                            in_offset=bass.IndirectOffsetOnAxis(ap=g_idx[v][:, j:j + 1], axis=0))\
                            .then_inc(s_g[v], 16)
                if products:
                    pool.wait_ge(s_si, e + 1)
                    count(pool, s_add, e * CT * 16)
                    for j in range(CT):
                        pool.wait_ge(s_y, e * CT + j + 1)
                        apart(pool, s_pass)
                        pool.indirect_dma_start(
                            out=dram["res"], out_offset=bass.IndirectOffsetOnAxis(ap=s_idx[u][:, j:j + 1], axis=0),
                            in_=y[:, j, :], in_offset=None, compute_op=ALU.add).then_inc(s_add, 16)

            pipeline(step)(pool)
            pool.wait_ge(s_add, E * CT * 16)

        @block.scalar
        def _(act):
            def step(e, u, slots, rows, products):
                v = 1 - u
                split = pieces((w1, w2), (w1h[v], w2h[v]), (w1l[v], w2l[v])) if rows else []
                if products:
                    act.wait_ge(s_b1, e + 1)
                for f in range(FC):
                    if products:
                        act.wait_ge(s_ph, e * FC + f + 1)
                        count(act, s_hl, e * FC + f - 1 if f >= 2 else e * FC)
                        act.activation(h[f % 2][:], ps_h[f % 2][:, :, 0:HALF], ACT.Gelu, bias=b1[u][:, f:f + 1],
                                       scale=1.0 / WS).then_inc(s_h, 1)
                        act.wait_ge(s_h, e * FC + f + 1)
                        if f == 0:
                            count(act, s_py, e * CT)
                        act.activation(hh[:, f, :], h[f % 2][:].rearrange("p a b -> p (a b)"), ACT.Copy)\
                            .then_inc(s_hh, 1)
                    if rows and f < len(split):
                        if f == 0:
                            act.wait_ge(s_w, (e + 2) * 32)
                            count(act, s_py, e * CT)
                        stage, high, low = split[f]
                        act.activation(high, stage, ACT.Copy, scale=WS).then_inc(s_wh, 1)
                    if rows and 0 <= f - FIRST < CT:
                        j = f - FIRST
                        act.wait_ge(s_px, (e + 1) * CT + j + 1)
                        act.activation(xh[v][:, :, j * P:(j + 1) * P], ps_x[j % 2], ACT.Copy).then_inc(s_xh, 1)
                if products:
                    for j in range(CT):
                        act.wait_ge(s_yb, e * CT + j + 1)
                        if j == 0:
                            count(act, s_add, e * CT * 16)
                        act.activation(y[:, j, :], yb[:, j, :], ACT.Copy, scale=gate[u][:, j:j + 1])\
                            .then_inc(s_y, 1)

            pipeline(step)(act)

        @block.vector
        def _(dve):
            dve.wait_ge(s_cst, 8)
            dve.tensor_copy(free[:], one_row[:]).then_inc(s_free, 1)
            for e in range(E):
                dve.wait_ge(s_free, e + 1)
                dve.tensor_tensor(elig[:, e, :], match[:, :, e], free[:], ALU.mult).then_inc(s_elig, 1)
                dve.wait_ge(s_elig, e + 1)
                dve.tensor_copy(elig16[:, e, :], elig[:, e, :]).then_inc(s_e16, 1)
                dve.tensor_tensor_scan(cum[:], one_row[:], elig[:, e, :], 0.0, ALU.mult, ALU.add).then_inc(s_cum, 1)
                dve.wait_ge(s_cum, e + 1)
                if e:
                    dve.wait_ge(s_ppos, e)
                dve.tensor_tensor(excl[:], cum[:], elig[:, e, :], ALU.subtract).then_inc(s_excl, 1)
                dve.wait_ge(s_ppos, e + 1)
                dve.tensor_copy(pos[:, e, :], ps_i[:, e * NT:(e + 1) * NT]).then_inc(s_pos, 1)
                dve.scalar_tensor_tensor(out=over[:], in0=ps_i[:, e * NT:(e + 1) * NT], scalar=float(CAP),
                                         in1=elig[:, e, :], op0=ALU.is_gt, op1=ALU.mult).then_inc(s_over, 1)
                dve.wait_ge(s_over, e + 1)
                dve.tensor_tensor(free[:], free[:], over[:], ALU.subtract).then_inc(s_free, 1)
            dve.wait_ge(s_free, E + 1)
            dve.wait_ge(s_pos, E)
            dve.tensor_scalar(fallen[:], free[:], -1.0, 1.0, ALU.mult, ALU.add).then_inc(s_fell, 1)
            dve.tensor_scalar(inside[:], pos[:], float(CAP), None, ALU.is_le).then_inc(s_in1, 1)
            dve.tensor_scalar(slot[:], pos[:], -1.0, None, ALU.add).then_inc(s_slot, 1)
            dve.wait_ge(s_in1, 1)
            dve.tensor_tensor(inside[:], inside[:], elig[:], ALU.mult).then_inc(s_in2, 1)
            dve.tensor_tensor(value[:], token1[:].unsqueeze(1).to_broadcast([P, E, NT]),
                              free[:].unsqueeze(1).to_broadcast([P, E, NT]), ALU.mult).then_inc(s_in2, 1)
            dve.wait_ge(s_slot, 1)
            dve.tensor_scalar(slot_lo[:], slot[:], P - 1, None, ALU.bitwise_and).then_inc(s_split, 1)
            dve.tensor_scalar(slot_hi[:], slot[:], P.bit_length() - 1, None, ALU.arith_shift_right)\
                .then_inc(s_split, 1)
            dve.wait_ge(s_in2, 2)
            dve.tensor_tensor(value[:], value[:], inside[:], ALU.mult).then_inc(s_value, 1)
            dve.wait_ge(s_split, 2)
            dve.tensor_copy(lo16[:], slot_lo[:]).then_inc(s_lohi, 1)
            dve.tensor_copy(hi16[:], slot_hi[:]).then_inc(s_lohi, 1)
            dve.wait_ge(s_fell, 1)
            dve.tensor_reduce(fallen_any[:], fallen[:], AX_X, ALU.max).then_inc(s_fsum, 1)
            dve.wait_ge(s_pb1, 1)
            dve.tensor_copy(b1T[:], ps_i[:, BT:BT + E * FC]).then_inc(s_b1T, 1)
            dve.wait_ge(s_pany, 1)
            dve.tensor_copy(fallen_n[:], ps_i[:, ANY:ANY + 1]).then_inc(s_any, 1)
            dve.wait_ge(s_b1T, 1)
            dve.wait_ge(s_value, 1)
            dve.wait_ge(s_lohi, 2)
            dve.wait_ge(s_ldb, 32)

            def of(table, e):
                return table[:, e, :] if isinstance(e, int) else \
                    table[:, bass.ds(e, 1), :].rearrange("p a b -> p (a b)")

            def step(e, u, slots, rows, products):
                v = 1 - u
                if slots:
                    count(dve, s_pidx, e + 1)
                    dve.tensor_tensor(at_lo[u][:], lane[:].unsqueeze(1).to_broadcast([P, NT, P]),
                                      of(lo16, e + 2).unsqueeze(2).to_broadcast([P, NT, P]), ALU.is_equal)\
                        .then_inc(s_atlo, 1)
                    dve.tensor_tensor(at_hi[u][:], tile_no[:].unsqueeze(1).to_broadcast([P, NT, CT]),
                                      of(hi16, e + 2).unsqueeze(2).to_broadcast([P, NT, CT]), ALU.is_equal)\
                        .then_inc(s_athi, 1)
                    dve.wait_ge(s_athi, e + 3)
                    dve.tensor_tensor(vhi[u][:], at_hi[u][:], of(value, e + 2).unsqueeze(2)
                                      .to_broadcast([P, NT, CT]), ALU.mult).then_inc(s_vhi, 1)
                split = pieces((w1, w2), (w1h[v], w2h[v]), (w1l[v], w2l[v])) if rows else []
                for f in range(FC):
                    if products:
                        dve.wait_ge(s_hh, e * FC + f + 1)
                        dve.tensor_tensor(hl[:, f, :], h[f % 2][:].rearrange("p a b -> p (a b)"), hh[:, f, :],
                                          ALU.subtract).then_inc(s_hl, 1)
                    if rows and f < len(split):
                        stage, high, low = split[f]
                        dve.wait_ge(s_wh, (e + 1) * 2 * WP + f + 1)
                        dve.scalar_tensor_tensor(out=low, in0=stage, scalar=WS, in1=high, op0=ALU.mult,
                                                 op1=ALU.subtract).then_inc(s_wl, 1)
                    if rows and 0 <= f - FIRST < CT:
                        j = f - FIRST
                        dve.wait_ge(s_xh, (e + 1) * CT + j + 1)
                        dve.tensor_tensor(xl[v][:, :, j * P:(j + 1) * P], ps_x[j % 2],
                                          xh[v][:, :, j * P:(j + 1) * P], ALU.subtract).then_inc(s_xl, 1)
                if rows:
                    count(dve, s_y, e * CT)
                    dve.tensor_copy(gate[v][:], xg[v][:, :, D + e + 1] if isinstance(e, int) else
                                    xg[v][:, :, bass.ds(D + 1 + e, 1)].rearrange("p a b -> p (a b)"))\
                        .then_inc(s_gate, 1)
                    dve.tensor_copy(b1[v][:], of(b1T[:].rearrange("p (e c) -> p e c", e=E), e + 1))\
                        .then_inc(s_b1, 1)
                if slots:
                    dve.wait_ge(s_pidx, e + 3)
                    dve.tensor_copy(of(who, e + 2), ps_i[:, IDX:IDX + CT]).then_inc(s_who, 1)
                    dve.tensor_scalar(empty_g[:], ps_i[:, IDX:IDX + CT], 0.0, None, ALU.is_equal).then_inc(s_emg, 1)
                    dve.wait_ge(s_emg, e + 3)
                    dve.wait_ge(s_who, e + 3)
                    if not (isinstance(e, int) and e < 0):
                        dve.wait_ge(s_g[u], (e - u) * (8 * CT) + 16 * CT)
                    dve.scalar_tensor_tensor(out=g_idx[u][:], in0=of(who, e + 2), scalar=-1.0, in1=empty_g[:],
                                             op0=ALU.add, op1=ALU.add).then_inc(s_gi, 1)
                if products:
                    dve.tensor_scalar(empty_s[:], of(who, e), 0.0, None, ALU.is_equal).then_inc(s_ems, 1)
                    dve.wait_ge(s_ems, e + 1)
                    dve.tensor_tensor(jump[:], empty_s[:], spare1[:], ALU.mult).then_inc(s_jmp, 1)
                    dve.wait_ge(s_jmp, e + 1)
                    count(dve, s_add, e * CT * 16)
                    dve.scalar_tensor_tensor(out=s_idx[u][:], in0=of(who, e), scalar=-1.0, in1=jump[:],
                                             op0=ALU.add, op1=ALU.add).then_inc(s_si, 1)
                    for j in range(CT):
                        dve.wait_ge(s_py, e * CT + j + 1)
                        if j == 0:
                            count(dve, s_y, e * CT)
                        dve.scalar_tensor_tensor(out=yb[:, j, :], in0=ps_y[(j + CT) % 2][:, 0:D], scalar=1.0 / WS,
                                                 in1=of(b2, e), op0=ALU.mult, op1=ALU.add).then_inc(s_yb, 1)

            pipeline(step)(dve)

        @block.tensor
        def _(pe):
            pe.wait_ge(s_cst, 8)
            pe.wait_ge(s_ldb, 32)
            pe.transpose(ps_i[:, BT:BT + E * FC], b1_in[:], ident[0:E * FC, 0:E * FC]).then_inc(s_pb1, 1)
            for e in range(E):
                out = ps_i[:, POS + e * NT:POS + (e + 1) * NT]
                pe.wait_ge(s_e16, e + 1)
                pe.matmul(out, tri[:], elig16[:, e, :], start=True, stop=False)
                pe.wait_ge(s_excl, e + 1)
                pe.matmul(out, ones16[:], excl[:], start=False, stop=True).then_inc(s_ppos, 1)
            pe.wait_ge(s_fsum, 1)
            pe.wait_ge(s_pos, E)
            pe.wait_ge(s_b1T, 1)
            pe.matmul(ps_i[:, ANY:ANY + 1], ones[:], fallen_any[:], start=True, stop=True).then_inc(s_pany, 1)
            pe.wait_ge(s_any, 1)

            def step(e, u, slots, rows, products):
                v = 1 - u
                if products:
                    pe.wait_ge(s_xl, (e + 1) * CT)
                    pe.wait_ge(s_wl, (e + 1) * 2 * WP)
                for f in range(FC):
                    if products:
                        if f >= 2:
                            pe.wait_ge(s_h, e * FC + f - 1)
                        for c in range(C):
                            hi, lo = w1h[u][:, c, f * P:(f + 1) * P], w1l[u][:, c, f * P:(f + 1) * P]
                            for k, (a, b) in enumerate(((hi, xh[u]), (hi, xl[u]), (lo, xh[u]))):
                                for t in range(2):
                                    last = pe.matmul(ps_h[f % 2][:, t, 0:HALF], a, b[:, c, t * HALF:(t + 1) * HALF],
                                                     start=(c == 0 and k == 0), stop=(c == C - 1 and k == 2))
                        last.then_inc(s_ph, 1)
                    if rows and 0 <= f - FIRST < CT:
                        j = f - FIRST
                        if j == 0:
                            pe.wait_ge(s_g[v], (e + 1 - v) * (8 * CT) + 16 * CT)
                            count(pe, s_yb, e * CT)
                        if j >= 2:
                            pe.wait_ge(s_xl, (e + 1) * CT + j - 1)
                        for c in range(C):
                            last = pe.transpose(ps_x[j % 2][:, c, :], xg[v][:, j, c * P:(c + 1) * P], ident[:])
                        last.then_inc(s_px, 1)
                if slots:
                    pe.wait_ge(s_vhi, e + 3)
                    pe.wait_ge(s_atlo, e + 3)
                    count(pe, s_emg, e + 2)
                    count(pe, s_who, e + 2)
                    for i in range(NT):
                        last = pe.matmul(ps_i[:, IDX:IDX + CT], at_lo[u][:, i, :], vhi[u][:, i, :],
                                         start=(i == 0), stop=(i == NT - 1))
                    last.then_inc(s_pidx, 1)
                if products:
                    for j in range(CT):
                        if j >= 2:
                            pe.wait_ge(s_yb, e * CT + j - 1)
                        elif rows:
                            pe.wait_ge(s_xl, (e + 2) * CT + j - 1)
                        for f in range(FC):
                            if j == 0:
                                pe.wait_ge(s_hl, e * FC + f + 1)
                            hi, lo = hh[:, f, j * P:(j + 1) * P], hl[:, f, j * P:(j + 1) * P]
                            for k, (a, b) in enumerate(((hi, w2h[u]), (hi, w2l[u]), (lo, w2h[u]))):
                                last = pe.matmul(ps_y[(j + CT) % 2][:, 0:D], a, b[:, f, :], start=(f == 0 and k == 0),
                                                 stop=(f == FC - 1 and k == 2))
                        last.then_inc(s_py, 1)

            pipeline(step)(pe)


def overflow_tokens(nc, S, ins, dram, keep):
    D, C, F, NT = S.D, S.C, S.F0, S.NT
    FC = F // P
    ident, tg, fallen = keep["ident"], keep["tg"], keep["fallen"]
    with ExitStack() as ctx:
        def sb(name, shape):
            return ctx.enter_context(nc.sbuf_tensor("f_" + name, shape, F32))

        def pb(name, shape):
            return ctx.enter_context(nc.psum_tensor("f_" + name, shape, F32))

        def sem(name):
            return nc.alloc_semaphore("f_" + name)

        w1 = sb("w1", [P, C, F]); b1 = sb("b1", [P, FC])
        w2 = sb("w2", [P, FC, D]); b2 = sb("b2", [P, D])
        fg = sb("fg", [P, NT])
        rows = sb("rows", [P, S.ROW]); res = sb("res", [P, D])
        xT = sb("xT", [P, C, P]); h = sb("h", [P, FC, P])
        yb = sb("yb", [P, D]); y = sb("y", [P, D]); new = sb("new", [P, D])
        ps_x = pb("ps_x", [P, 512]); ps_h = pb("ps_h", [P, FC, P]); ps_y = pb("ps_y", [P, 512])
        s_w = sem("w"); s_fg = sem("fg"); s_rows = sem("rows"); s_res = sem("res"); s_px = sem("px"); s_xT = sem("xT")
        s_ph = sem("ph"); s_h = sem("h"); s_py = sem("py"); s_yb = sem("yb"); s_y = sem("y"); s_new = sem("new")
        s_store = sem("store"); s_passs = sem("passs")
        rows_t = dram["rows"].rearrange("(t p) d -> t p d", p=P)
        res_t = dram["res"][0:S.N, :].rearrange("(t p) d -> t p d", p=P)
        block = ctx.enter_context(nc.Block())

        @block.sync
        def _(sp):
            with sp.If(sp.value_load(keep["fallen_n"][0:1, 0:1]) > 0):
                sp.dma_start(w1[:], chunks(ins["L0_ffn_fw1"])).then_inc(s_w, 16)
                sp.dma_start(w2[:], chunks(ins["L0_ffn_fw2"])).then_inc(s_w, 16)
                sp.dma_start(b1[:], col(ins["L0_ffn_fb1"])).then_inc(s_w, 16)
                sp.dma_start(b2[:], row(ins["L0_ffn_fb2"])).then_inc(s_w, 16)

                def tile(i):
                    sp.dma_start(rows[:], rows_t[i]).then_inc(s_rows, 16)
                    sp.dma_start(res[:], res_t[i]).then_inc(s_res, 16)
                    sp.wait_ge(s_new, i + 1)
                    sp.dma_start(res_t[i], new[:]).then_inc(s_store, 16)
                    sp.wait_ge(s_store, (i + 1) * 16)
                    apart(sp, s_passs)

                tile(0)
                with sp.Fori(1, NT - 1) as i:
                    tile(i)
                tile(NT - 1)

        @block.scalar
        def _(act):
            with act.If(act.value_load(keep["fallen_n"][0:1, 0:1]) > 0):
                act.wait_ge(s_w, 64)
                with act.Fori(0, NT) as i:
                    act.wait_ge(s_px, i + 1)
                    act.activation(xT[:].rearrange("p c t -> p (c t)"), ps_x[:, 0:C * P], ACT.Copy).then_inc(s_xT, 1)
                    act.wait_ge(s_ph, i + 1)
                    for f in range(FC):
                        act.activation(h[:, f, :], ps_h[:, f, :], ACT.Gelu, bias=b1[:, f:f + 1]).then_inc(s_h, 1)

        @block.vector
        def _(dve):
            with dve.If(dve.value_load(keep["fallen_n"][0:1, 0:1]) > 0):
                dve.wait_ge(s_w, 64)
                dve.tensor_scalar(fg[:], fallen[:], tg[:, 2:3], None, ALU.mult).then_inc(s_fg, 1)
                dve.wait_ge(s_fg, 1)
                with dve.Fori(0, NT) as i:
                    dve.wait_ge(s_py, i + 1)
                    dve.tensor_tensor(yb[:], ps_y[:, 0:D], b2[:], ALU.add).then_inc(s_yb, 1)
                    dve.wait_ge(s_yb, i + 1)
                    dve.tensor_tensor(y[:], yb[:], fg[:, bass.ds(i, 1)].to_broadcast([P, D]), ALU.mult)\
                        .then_inc(s_y, 1)
                    dve.wait_ge(s_y, i + 1)
                    dve.wait_ge(s_res, (i + 1) * 16)
                    dve.tensor_tensor(new[:], res[:], y[:], ALU.add).then_inc(s_new, 1)

        @block.tensor
        def _(pe):
            with pe.If(pe.value_load(keep["fallen_n"][0:1, 0:1]) > 0):
                pe.wait_ge(s_w, 64)
                with pe.Fori(0, NT) as i:
                    pe.wait_ge(s_rows, (i + 1) * 16)
                    for c in range(C):
                        last = pe.transpose(ps_x[:, c * P:(c + 1) * P], rows[:, c * P:(c + 1) * P], ident[:])
                    last.then_inc(s_px, 1)
                    pe.wait_ge(s_xT, i + 1)
                    for f in range(FC):
                        for c in range(C):
                            last = pe.matmul(ps_h[:, f, :], w1[:, c, f * P:(f + 1) * P], xT[:, c, :],
                                             start=(c == 0), stop=(c == C - 1))
                    last.then_inc(s_ph, 1)
                    pe.wait_ge(s_h, (i + 1) * FC)
                    for f in range(FC):
                        last = pe.matmul(ps_y[:, 0:D], h[:, f, :], w2[:, f, :], start=(f == 0), stop=(f == FC - 1))
                    last.then_inc(s_py, 1)


def attention_dilated(nc, S, ins, dram, keep, out):
    B, T, D, C, E, H, HD, NT = S.B, S.T, S.D, S.C, S.E, S.H, S.HD, S.NT
    QK = P + T
    BR = 3
    W = BR * (HD + 1)
    HH = H // 2
    SCALE = float(HD) ** -0.5
    assert H * HD == D and HH * W <= 512 and 3 * HD <= 64 and P % 4 == 0
    assert S.T <= 256
    ident, tg, wT, prob = keep["ident"], keep["tg"], keep["wT_out"], keep["prob"]
    with ExitStack() as ctx:
        def sb(name, shape, dt=F32):
            return ctx.enter_context(nc.sbuf_tensor("c_" + name, shape, dt))

        def two(name, shape, dt=F32):
            return [sb(f"{name}{u}", shape, dt) for u in range(2)]

        def pb(name):
            return ctx.enter_context(nc.psum_tensor("c_" + name, [P, 512], F32))

        sem = stage_semaphores(nc, ctx, "c_")
        s_pass = sem("pass"); s_passd = sem("passd"); s_passs = sem("passs")

        half = sb("half", [P, 2])
        mask = sb("mask", [P, QK])
        lane_i = sb("lane_i", [P, 1], I32)
        mod_i = sb("mod_i", [P, 2], I32)
        mod_f = sb("mod_f", [P, 2])
        group = sb("group", [P, 2, H])
        member = sb("member", [P, H, BR])
        bq = sb("bq", [P, C])
        bqs = sb("bqs", [P, C])
        bo = sb("bo", [P, D])
        bot = sb("bot", [P, D])
        br = sb("br", [P, E])
        wr = sb("wr", [P, C, E])

        x_in = two("x_in", [P, 2, D])
        xb = two("xb", [P, 2, D])
        st = two("st", [P, 2, 6]); mv = two("mv", [P, 2, 2]); var = two("var", [P, 2])
        rstd = two("rstd", [P, 2]); nmr = two("nmr", [P, 2])
        xn = two("xn", [P, 2, D])
        xT = sb("xT", [P, C, T])
        qf = sb("qf", [P, C, T])
        qh = two("qh", [P, C, T], F16)
        ql = two("ql", [P, C, T], F16)
        qs = two("qs", [P, HH, T], F16)
        ks = two("ks", [P, HH, T], F16)
        v_in = two("v_in", [P, 2, D])
        vx = two("vx", [P, 2, H, BR, HD + 1])
        sn = [sb(f"sn{k}", [P, QK]) for k in range(4)]
        pr = [sb(f"pr{k}", [P, QK]) for k in range(4)]
        prT = [sb(f"prT{k}", [P, QK]) for k in range(2)]
        nm = two("nm", [P, 2, H])
        nmc = sb("nmc", [P, 2, H])
        em = sb("em", [P, 2, H])
        acc = two("acc", [P, 2, H, BR, HD + 1])
        prod = sb("prod", [P, 2 * H, BR])
        live = sb("live", [P, 2 * H, BR])
        zl = sb("zl", [P, 2 * H, BR])
        zs = sb("zs", [P, 2 * H])
        none = sb("none", [P, 2 * H])
        zs1 = sb("zs1", [P, 2 * H])
        rz = sb("rz", [P, 2 * H])
        zc = sb("zc", [P, 2 * H, BR])
        rc = sb("rc", [P, 2 * H, BR])
        am = sb("am", [P, 2 * H, BR])
        an = sb("an", [P, 2 * H, BR])
        al = sb("al", [P, 2 * H, BR])
        aw = sb("aw", [P, 2 * H, BR])
        mix = sb("mix", [P, 2 * H, BR, HD])
        mix2 = sb("mix2", [P, 2 * H, HD])
        o = sb("o", [P, 2, D])
        oT = sb("oT", [P, C, T])
        x3 = two("x3", [P, 2, D])
        st3 = two("st3", [P, 2, 6]); mv3 = two("mv3", [P, 2, 2]); var3 = two("var3", [P, 2])
        rstd3 = two("rstd3", [P, 2]); nmr3 = two("nmr3", [P, 2])
        rows = two("rows", [P, 2, S.ROW])
        x3T = sb("x3T", [P, C, T])
        lg = sb("lg", [P, 2, E]); lmx = sb("lmx", [P, 2]); lgs = sb("lgs", [P, 2, E])
        le = sb("le", [P, 2, E]); lsum = sb("lsum", [P, 2]); lrec = sb("lrec", [P, 2])
        lp = sb("lp", [P, 2, E])

        ps_s = [pb(f"ps_s{k}") for k in range(2)]
        ps_t = [pb(f"ps_t{k}") for k in range(2)]
        ps_n = [pb(f"ps_n{k}") for k in range(2)]
        ps_a, ps_b = pb("ps_a"), pb("ps_b")

        s_cst = sem("cst"); s_ldb = sem("ldb"); s_mod = sem("mod"); s_modf = sem("modf"); s_mem = sem("mem")
        s_bias = sem("bias"); s_one = sem("one")
        s_ldx = [sem("ldx0"), sem("ldx1")]; s_ldk = [sem("ldk0"), sem("ldk1")]; s_ldv = [sem("ldv0"), sem("ldv1")]
        s_st = sem("st"); s_mv = sem("mv"); s_var = sem("var"); s_rstd = sem("rstd"); s_mr = sem("mr")
        s_nmr = sem("nmr"); s_xn = sem("xn"); s_xb = sem("xb"); s_vx = sem("vx")
        s_pxt = sem("pxt"); s_xT = sem("xT"); s_pq = sem("pq"); s_qf = sem("qf"); s_qh = sem("qh"); s_ql = sem("ql")
        s_qst = [sem("qst0"), sem("qst1")]; s_ldq = [sem("ldq0"), sem("ldq1")]
        s_ps = sem("ps"); s_sn = sem("sn"); s_pr = sem("pr"); s_ppt = sem("ppt"); s_prT0 = sem("prT0")
        s_prT1 = sem("prT1")
        s_pn = sem("pn"); s_acc = sem("acc")
        s_nmc = sem("nmc"); s_em = sem("em"); s_prod = sem("prod"); s_live = sem("live"); s_zl = sem("zl")
        s_zs = sem("zs"); s_none = sem("none"); s_zs1 = sem("zs1"); s_rz = sem("rz"); s_zc = sem("zc")
        s_rc = sem("rc"); s_am = sem("am"); s_an = sem("an"); s_al = sem("al"); s_aw = sem("aw")
        s_mix = sem("mix"); s_mix2 = sem("mix2"); s_o = sem("o")
        s_pot = sem("pot"); s_oT = sem("oT"); s_po = sem("po"); s_x3 = sem("x3"); s_xst = [sem("xst0"), sem("xst1")]
        s_st3 = sem("st3"); s_mv3 = sem("mv3"); s_var3 = sem("var3"); s_rstd3 = sem("rstd3"); s_mr3 = sem("mr3")
        s_nmr3 = sem("nmr3"); s_xn3 = sem("xn3"); s_px3 = sem("px3"); s_x3T = sem("x3T"); s_plg = sem("plg")
        s_lg = sem("lg"); s_lmx = sem("lmx"); s_lgs = sem("lgs"); s_le = sem("le"); s_lsum = sem("lsum")
        s_lrec = sem("lrec"); s_lp = sem("lp"); s_prob = sem("prob"); s_gate = sem("gate")
        s_rst = [sem("rst0"), sem("rst1")]

        def pipeline(step):
            def run(eng):
                step(-1, 1, True, False, False)
                step(0, 0, True, True, False)
                step(1, 1, True, True, True)
                with eng.Fori(0, B // 2 - 2) as i:
                    step(i * 2 + 2, 0, True, True, True)
                    step(i * 2 + 3, 1, True, True, True)
                step(B - 2, 0, True, True, True)
                step(B - 1, 1, False, True, True)
                step(B, 0, False, False, True)
            return run

        def after(eng, what, n, back=0, per=1, extra=0):
            if not isinstance(n, int) or n >= back:
                eng.wait_ge(what, (n - back) * per + per + extra)

        def landed(eng, pair, n, u, back=0, per=16):
            if not isinstance(n, int) or n >= back:
                par = (u + back) % 2
                eng.wait_ge(pair[par], (n - back - par) * (per // 2) + per)

        def head(n, u, k, front, heads, back):
            if k >= H:
                return (n + 1, 1 - u, k - H) if front else None
            if k < 0:
                return (n - 1, 1 - u, k + H) if back else None
            return (n, u, k) if heads else None

        def heads_done(eng, what, n, k, back=0, per=1):
            if not isinstance(n, int) or n * H + k >= back:
                eng.wait_ge(what, (n * H + k - back + 1) * per)

        def halves(bank):
            return bank[:].rearrange("p (c t) -> p c t", c=2)

        block = ctx.enter_context(nc.Block())
        res_t = dram["res"][0:S.N, :].rearrange("(b j p) d -> b p j d", b=B, p=P)
        rows_t = dram["rows"].rearrange("(b j p) d -> b p j d", b=B, p=P)
        out_t = out.rearrange("b (j p) d -> b p j d", p=P)

        def stacked(part):
            return part.rearrange("(b r d) t -> r d b t", r=2, d=HD)

        @block.sync
        def _(sp):
            sp.dma_start(bq[:], col(ins["L1_xattn_bq"])).then_inc(s_ldb, 16)
            sp.dma_start(bo[:], row(ins["L1_xattn_bo"])).then_inc(s_ldb, 16)
            sp.dma_start(br[:], row(ins["L1_ffn_br"])).then_inc(s_ldb, 16)
            sp.dma_start(wr[:], chunks(ins["L1_ffn_Wr"])).then_inc(s_ldb, 16)

            def load_x(n, u):
                sp.dma_start(x_in[u][:], res_t[n]).then_inc(s_ldx[u], 16)

            def load_kv(n, u):
                sp.dma_start(v_in[u][:], dram["v"][n]).then_inc(s_ldv[u], 16)
                for part, which in enumerate((0, 1, 0)):
                    for r in range(2):
                        a = 64 * r + HD * part
                        sp.dma_start(ks[u][a:a + HD, :, :], stacked(dram["kT"][n, which])[r]).then_inc(s_ldk[u], 16)

            load_x(0, 0)

            def step(n, u, front, heads, back):
                v = 1 - u
                if front:
                    if not (isinstance(n, int) and n + 2 >= B):
                        after(sp, s_xn, n, 0, 2)
                        apart(sp, s_passs)
                        after(sp, s_xb, n)
                        load_x(n + 2, u)
                    after(sp, s_vx, n, 1, 2)
                    apart(sp, s_passs)
                    heads_done(sp, s_ps, n - 1, H - 1)
                    load_kv(n + 1, v)
                    after(sp, s_qh, n, -1)
                    after(sp, s_ql, n, -1)
                    sp.dma_start(dram["q"][v, 0].rearrange("(c p) t -> p c t", p=P), qh[v][:]).then_inc(s_qst[v], 16)
                    sp.dma_start(dram["q"][v, 1].rearrange("(c p) t -> p c t", p=P), ql[v][:]).then_inc(s_qst[v], 16)
                    landed(sp, s_qst, n, u, -1, 32)
                    for part, which in enumerate((0, 0, 1)):
                        for r in range(2):
                            a = 64 * r + HD * part
                            sp.dma_start(qs[v][a:a + HD, :, :], stacked(dram["q"][v, which])[r])\
                                .then_inc(s_ldq[v], 16)
                if back:
                    after(sp, s_x3, n, 1, 2)
                    sp.dma_start(out_t[n - 1], x3[v][:]).then_inc(s_xst[v], 16)
                    after(sp, s_gate, n, 1)
                    sp.dma_start(rows_t[n - 1], rows[v][:]).then_inc(s_rst[v], 16)

            pipeline(step)(sp)
            for u in range(2):
                for pair, per in ((s_qst, 32), (s_xst, 16), (s_rst, 16)):
                    sp.wait_ge(pair[u], per * B // 2)

        @block.gpsimd
        def _(pool):
            pool.memset(half[:], -0.5).then_inc(s_cst, 1)
            pool.memset(mask[:], 0.0).then_inc(s_cst, 1)
            pool.memset(member[:], 1.0).then_inc(s_cst, 1)
            pool.iota(lane_i[:], pattern=[[0, 1]], base=0, channel_multiplier=1).then_inc(s_cst, 1)
            pool.iota(group[:, 0, :], pattern=[[1, 2], [0, H // 2]], base=0, channel_multiplier=0,
                      allow_small_or_imprecise_dtypes=True).then_inc(s_cst, 1)
            pool.iota(group[:, 1, :], pattern=[[1, 4], [0, H // 4]], base=0, channel_multiplier=0,
                      allow_small_or_imprecise_dtypes=True).then_inc(s_cst, 1)
            pool.wait_ge(s_cst, 6)
            for a in (0, T):
                pool.affine_select(out=mask[:, a:a + P], in_=mask[:, a:a + P], compare_op=ALU.is_ge, fill=NEG,
                                   base=0, pattern=[[-1, P]], channel_multiplier=1).then_inc(s_cst, 1)
            pool.wait_ge(s_mem, 2)
            for u in range(2):
                for j in range(2):
                    pool.tensor_copy(vx[u][:, j, :, :, HD], member[:]).then_inc(s_one, 1)

            def layernorm_scale(n, s_v, var_, rstd_, s_r, mv_, nmr_, s_m, s_n):
                after(pool, s_v, n)
                pool.tensor_tensor(rstd_[:], var_[:], half[:], ALU.pow).then_inc(s_r, 1)
                after(pool, s_r, n)
                pool.tensor_tensor(nmr_[:], mv_[:, :, 0], rstd_[:], ALU.mult).then_inc(s_m, 1)
                after(pool, s_m, n)
                apart(pool, s_pass)
                pool.tensor_scalar(nmr_[:], nmr_[:], -1.0, None, ALU.mult).then_inc(s_n, 1)

            def step(n, u, front, heads, back):
                v = 1 - u
                if front:
                    layernorm_scale(n + 1, s_var, var[v], rstd[v], s_rstd, mv[v], nmr[v], s_mr, s_nmr)
                if front:
                    landed(pool, s_ldv, n, u, -1)
                    heads_done(pool, s_pn, n - 1, H - 1)
                    apart(pool, s_pass)
                    for j in range(2):
                        vv = v_in[v][:, j, :].rearrange("p (h d) -> p h d", h=H)
                        pool.tensor_copy(vx[v][:, j, :, 0, 0:HD], vv)
                        for b in range(1, BR):
                            last = pool.tensor_tensor(vx[v][:, j, :, b, 0:HD], vv,
                                                      member[:, :, b:b + 1].to_broadcast([P, H, HD]), ALU.mult)
                        last.then_inc(s_vx, 1)
                m = n - 1
                if back:
                    layernorm_scale(m, s_var3, var3[v], rstd3[v], s_rstd3, mv3[v], nmr3[v], s_mr3, s_nmr3)
                if front:
                    landed(pool, s_ldx, n, u, -1)
                    after(pool, s_x3, n, 1, 2)
                    pool.tensor_tensor(xb[v][:], x_in[v][:], bot[:].unsqueeze(1).to_broadcast([P, 2, D]),
                                       ALU.add).then_inc(s_xb, 1)
                if back:
                    after(pool, s_lmx, m)
                    pool.tensor_tensor(lgs[:], lg[:], lmx[:].unsqueeze(2).to_broadcast([P, 2, E]), ALU.add)\
                        .then_inc(s_lgs, 1)
                    after(pool, s_lrec, m)
                    pool.tensor_tensor(lp[:], le[:], lrec[:].unsqueeze(2).to_broadcast([P, 2, E]), ALU.mult)\
                        .then_inc(s_lp, 1)
                    after(pool, s_lp, m)
                    pool.tensor_copy(prob[:, bass.ds(m * 2, 2), :], lp[:]).then_inc(s_prob, 1)
                    pool.tensor_scalar(rows[v][:, :, D:S.ROW], lp[:], tg[:, 3:4], None, ALU.mult).then_inc(s_gate, 1)

            pipeline(step)(pool)

        @block.scalar
        def _(act):
            def normalise(n, s_n, rstd_, nmr_, src, dst, s_done):
                after(act, s_n, n)
                for j in range(2):
                    act.activation(dst[:, j, 0:D], src[:, j, :], ACT.Identity, bias=nmr_[:, j:j + 1],
                                   scale=rstd_[:, j:j + 1]).then_inc(s_done, 1)

            def exps(n, u, k):
                heads_done(act, s_sn, n, k, 0, 2)
                heads_done(act, s_ppt, n, k, 4)
                for q, (a, b) in enumerate(((0, P), (P, QK))):
                    act.activation(pr[k % 4][:, a:b], sn[k % 4][:, a:b], ACT.Exp, bias=nm[u][:, q, k:k + 1],
                                   scale=-1.0).then_inc(s_pr, 1)

            def sums(n, u, part):
                heads_done(act, s_pn, n, (part + 1) * HH - 1)
                if part == 0:
                    after(act, s_mix, n, 2, BR)
                for q in range(2):
                    act.activation(acc[u][:, q, part * HH:(part + 1) * HH, :, :].rearrange("p h b d -> p (h b d)"),
                                   ps_n[q][:, 0:HH * W], ACT.Copy).then_inc(s_acc, 1)

            act.wait_ge(s_bias, 2)

            def step(n, u, front, heads, back):
                v = 1 - u
                for k in range(H):
                    ahead = head(n, u, k + 1, front, heads, back)
                    if ahead:
                        exps(*ahead)
                    if heads and k % 2 == 1:
                        heads_done(act, s_ppt, n, k)
                        heads_done(act, s_pn, n, k, 2)
                        act.activation(prT[k % 2][:], ps_t[k % 2][:, 0:QK], ACT.Copy).then_inc(s_prT1, 1)
                    if front and k == 1:
                        if not (isinstance(n, int) and n < 1):
                            after(act, s_pxt, n, 1)
                        normalise(n + 1, s_nmr, rstd[v], nmr[v], x_in[v], xn[v], s_xn)
                    if front and k == 3:
                        after(act, s_pxt, n, -1)
                        after(act, s_pq, n)
                        act.activation(xT[:], halves(ps_a), ACT.Copy).then_inc(s_xT, 1)
                    if front and k == 5:
                        after(act, s_pq, n, -1)
                        after(act, s_ql, n)
                        for c in range(C):
                            last = act.activation(qf[:, c, :], ps_b[:, c * T:(c + 1) * T], ACT.Identity,
                                                  bias=bqs[:, c:c + 1], scale=SCALE)
                        last.then_inc(s_qf, 1)
                        after(act, s_qf, n, -1)
                        if not (isinstance(n, int) and n < 1):
                            landed(act, s_qst, n, u, 1, 32)
                        act.activation(qh[v][:], qf[:], ACT.Copy).then_inc(s_qh, 1)
                    if heads and k == HH:
                        sums(n, u, 0)
                    if back:
                        m = n - 1
                        if k == 0:
                            sums(m, v, 1)
                        if k == 1:
                            after(act, s_nmc, m)
                            after(act, s_prod, m, 1)
                            act.activation(em[:], nmc[:], ACT.Exp, scale=-1.0).then_inc(s_em, 1)
                        if k == 7:
                            after(act, s_pot, m)
                            after(act, s_po, m, 1)
                            act.activation(oT[:], halves(ps_a), ACT.Copy).then_inc(s_oT, 1)
                        if k == 11:
                            landed(act, s_rst, m, v, 2)
                            after(act, s_x3, m, 0, 2)
                            normalise(m, s_nmr3, rstd3[v], nmr3[v], x3[v], rows[v], s_xn3)
                        if k == 12:
                            after(act, s_px3, m)
                            after(act, s_plg, m, 1)
                            act.activation(x3T[:], halves(ps_a), ACT.Copy).then_inc(s_x3T, 1)
                        if k == 15:
                            after(act, s_lgs, m)
                            after(act, s_lp, m, 1)
                            act.activation(le[:], lgs[:], ACT.Exp).then_inc(s_le, 1)

            pipeline(step)(act)

        @block.vector
        def _(dve):
            dve.wait_ge(s_cst, 8)
            dve.tensor_scalar(mod_i[:, 0:1], lane_i[:], 1, None, ALU.bitwise_and).then_inc(s_mod, 1)
            dve.tensor_scalar(mod_i[:, 1:2], lane_i[:], 3, None, ALU.bitwise_and).then_inc(s_mod, 1)
            dve.wait_ge(s_mod, 2)
            dve.tensor_copy(mod_f[:], mod_i[:]).then_inc(s_modf, 1)
            dve.wait_ge(s_modf, 1)
            for k in range(2):
                dve.tensor_scalar(member[:, :, k + 1], group[:, k, :], mod_f[:, k:k + 1], None, ALU.is_equal)\
                    .then_inc(s_mem, 1)
            dve.wait_ge(s_ldb, 64)
            dve.tensor_scalar(bqs[:], bq[:], SCALE, None, ALU.mult).then_inc(s_bias, 1)
            dve.tensor_scalar(bot[:], bo[:], tg[:, 1:2], None, ALU.mult).then_inc(s_bias, 1)
            dve.wait_ge(s_mem, 2)

            def stats(n, src, st_, s_st_, mv_, s_mv_, var_, s_var_):
                for j in range(2):
                    dve.bn_stats(st_[:, j, :], src[:, j, :]).then_inc(s_st_, 1)
                after(dve, s_st_, n, 0, 2)
                apart(dve, s_passd)
                for j in range(2):
                    dve.bn_aggr(mv_[:, j, :], st_[:, j, :]).then_inc(s_mv_, 1)
                after(dve, s_mv_, n, 0, 2)
                dve.tensor_scalar(var_[:], mv_[:, :, 1], EPS, None, ALU.add).then_inc(s_var_, 1)

            everywhere = member[:].unsqueeze(1).to_broadcast([P, 2, H, BR])

            def pairs(t):
                return t[:].rearrange("p (q h) b -> p q h b", q=2)

            def maxima(n, u, k):
                heads_done(dve, s_ps, n, k)
                heads_done(dve, s_pr, n, k, 4, 2)
                if k == 0:
                    after(dve, s_nmc, n, 2)
                apart(dve, s_passd)
                for q, (a, b) in enumerate(((0, P), (P, QK))):
                    dve.tensor_tensor_reduce(sn[k % 4][:, a:b], ps_s[k % 2][:, a:b], mask[:, a:b], -1.0, 3.0e38,
                                             ALU.add, ALU.min, nm[u][:, q, k:k + 1]).then_inc(s_sn, 1)

            def step(n, u, front, heads, back):
                v = 1 - u
                m = n - 1
                for k in range(H):
                    ahead = head(n, u, k + 2, front, heads, back)
                    if ahead:
                        maxima(*ahead)
                    if heads and k % 2 == 0:
                        heads_done(dve, s_ppt, n, k)
                        heads_done(dve, s_pn, n, k, 2)
                        dve.tensor_copy(prT[k % 2][:], ps_t[k % 2][:, 0:QK]).then_inc(s_prT0, 1)
                    if front and k == 0:
                        landed(dve, s_ldx, n, u, -1)
                        after(dve, s_nmr, n, 1)
                        stats(n + 1, x_in[v], st[v], s_st, mv[v], s_mv, var[v], s_var)
                    if front and k == 6:
                        after(dve, s_qh, n, -1)
                        if not (isinstance(n, int) and n < 1):
                            landed(dve, s_qst, n, u, 1, 32)
                        dve.tensor_tensor(ql[v][:], qf[:], qh[v][:], ALU.subtract).then_inc(s_ql, 1)
                    if back:
                        zb = acc[v][:, :, :, :, HD]
                        if k == 0:
                            heads_done(dve, s_sn, m, H - 1, 0, 2)
                            after(dve, s_em, m, 1)
                            dve.tensor_scalar(nmc[:], nm[v][:], -80.0, None, ALU.max).then_inc(s_nmc, 1)
                        if k == 2:
                            after(dve, s_acc, m, 0, 4)
                            after(dve, s_am, m, 1)
                            dve.tensor_scalar(pairs(zc), zb, 1e-37, float(BR), ALU.max, ALU.mult).then_inc(s_zc, 1)
                            after(dve, s_em, m)
                            after(dve, s_live, m, 1)
                            dve.tensor_tensor(pairs(prod), zb, em[:].unsqueeze(3).to_broadcast([P, 2, H, BR]),
                                              ALU.mult).then_inc(s_prod, 1)
                            after(dve, s_zc, m)
                            dve.reciprocal(rc[:], zc[:]).then_inc(s_rc, 1)
                            after(dve, s_prod, m)
                            after(dve, s_al, m, 1)
                            dve.scalar_tensor_tensor(out=pairs(live), in0=pairs(prod), scalar=1.0, in1=everywhere,
                                                     op0=ALU.not_equal, op1=ALU.mult).then_inc(s_live, 1)
                            after(dve, s_rc, m)
                            after(dve, s_an, m, 1)
                            dve.tensor_tensor(pairs(am), pairs(rc), everywhere, ALU.mult).then_inc(s_am, 1)
                            after(dve, s_live, m)
                            dve.tensor_tensor(pairs(zl), zb, pairs(live), ALU.mult).then_inc(s_zl, 1)
                        if k == 3:
                            after(dve, s_zl, m)
                            after(dve, s_zs1, m, 1)
                            dve.tensor_reduce(zs[:], zl[:], AX_X, ALU.add).then_inc(s_zs, 1)
                            after(dve, s_zs, m)
                            dve.tensor_scalar(none[:], zs[:], 0.0, None, ALU.is_equal).then_inc(s_none, 1)
                            after(dve, s_none, m)
                            after(dve, s_rz, m, 1)
                            dve.tensor_tensor(zs1[:], zs[:], none[:], ALU.add).then_inc(s_zs1, 1)
                            after(dve, s_am, m)
                            dve.tensor_tensor(an[:], am[:], none[:].unsqueeze(2).to_broadcast([P, 2 * H, BR]),
                                              ALU.mult).then_inc(s_an, 1)
                            after(dve, s_zs1, m)
                            dve.reciprocal(rz[:], zs1[:]).then_inc(s_rz, 1)
                            after(dve, s_rz, m)
                            dve.tensor_tensor(al[:], live[:], rz[:].unsqueeze(2).to_broadcast([P, 2 * H, BR]),
                                              ALU.mult).then_inc(s_al, 1)
                            after(dve, s_al, m)
                            after(dve, s_an, m)
                            dve.tensor_tensor(aw[:], al[:], an[:], ALU.add).then_inc(s_aw, 1)
                        if k == 4:
                            after(dve, s_aw, m)
                            for b in range(BR):
                                dve.tensor_tensor(mix[:, :, b, :],
                                                  acc[v][:, :, :, b, 0:HD].rearrange("p q h d -> p (q h) d"),
                                                  aw[:, :, b:b + 1].to_broadcast([P, 2 * H, HD]), ALU.mult)\
                                    .then_inc(s_mix, 1)
                        if k == 5:
                            after(dve, s_mix, m, 0, BR)
                            dve.tensor_tensor(mix2[:], mix[:, :, 0, :], mix[:, :, 1, :], ALU.add).then_inc(s_mix2, 1)
                            after(dve, s_mix2, m)
                            after(dve, s_pot, m, 1)
                            dve.tensor_tensor(o[:].rearrange("p q (h d) -> p (q h) d", h=H), mix2[:],
                                              mix[:, :, 2, :], ALU.add).then_inc(s_o, 1)
                        if k == 9:
                            after(dve, s_po, m)
                            after(dve, s_xb, m)
                            landed(dve, s_xst, m, v, 2)
                            after(dve, s_xn3, m, 2, 2)
                            for j in range(2):
                                dve.scalar_tensor_tensor(out=x3[v][:, j, :], in0=ps_b[:, j * D:(j + 1) * D],
                                                         scalar=tg[:, 1:2], in1=xb[v][:, j, :],
                                                         op0=ALU.mult, op1=ALU.add).then_inc(s_x3, 1)
                            after(dve, s_x3, m, 0, 2)
                            after(dve, s_nmr3, m, 2)
                            stats(m, x3[v], st3[v], s_st3, mv3[v], s_mv3, var3[v], s_var3)
                        if k == 14:
                            after(dve, s_plg, m)
                            after(dve, s_lgs, m, 1)
                            dve.tensor_tensor(lg[:], ps_b[:, 0:2 * E].rearrange("p (j e) -> p j e", j=2),
                                              br[:].unsqueeze(1).to_broadcast([P, 2, E]), ALU.add).then_inc(s_lg, 1)
                            after(dve, s_lg, m)
                            dve.tensor_reduce(lmx[:], lg[:], AX_X, ALU.max, negate=True).then_inc(s_lmx, 1)
                        if k == 15:
                            after(dve, s_le, m)
                            dve.tensor_reduce(lsum[:], le[:], AX_X, ALU.add).then_inc(s_lsum, 1)
                            after(dve, s_lsum, m)
                            after(dve, s_lp, m, 1)
                            dve.reciprocal(lrec[:], lsum[:]).then_inc(s_lrec, 1)

            pipeline(step)(dve)

        @block.tensor
        def _(pe):
            def turn(bank, src):
                for r in range(2):
                    for c in range(2):
                        last = pe.transpose(bank[:, c * T + r * P:c * T + (r + 1) * P],
                                            src[:, r, c * P:(c + 1) * P], ident[:])
                return last

            def product(bank, lhs, rhs):
                for r in range(2):
                    for c in range(C):
                        last = pe.matmul(bank[:, r * D:(r + 1) * D], lhs[:, c, r * P:(r + 1) * P], rhs[:, c, :],
                                         start=(c == 0), stop=(c == C - 1))
                return last

            def scores(n, u, k):
                if k == 0:
                    landed(pe, s_ldq, n, u, 0, 96)
                    landed(pe, s_ldk, n, u, 0, 96)
                heads_done(pe, s_sn, n, k, 2, 2)
                a = 64 * (k % 2)
                for q, (c, keys) in enumerate(((0, P), (P, T))):
                    last = pe.matmul(ps_s[k % 2][:, c:c + keys], qs[u][a:a + 3 * HD, k // 2, q * P:(q + 1) * P],
                                     ks[u][a:a + 3 * HD, k // 2, 0:keys], start=True, stop=True)
                last.then_inc(s_ps, 1)

            def turned(n, u, k):
                heads_done(pe, s_pr, n, k, 0, 2)
                copied(n, k, 2)
                for a in range(0, QK, P):
                    last = pe.transpose(ps_t[k % 2][:, a:a + P], pr[k % 4][:, a:a + P], ident[:])
                last.then_inc(s_ppt, 1)

            def copied(n, k, back=0):
                if not isinstance(n, int) or n * H + k >= back:
                    pe.wait_ge(s_prT1 if k % 2 else s_prT0, n * HH + (k - k % 2 - back) // 2 + 1)

            def weighted(n, u, k):
                copied(n, k)
                if k == 0:
                    after(pe, s_vx, n, 0, 2)
                if k % HH == 0:
                    if k:
                        after(pe, s_acc, n, 0, 4, -2)
                    else:
                        after(pe, s_acc, n, 1, 4)
                o = (k % HH) * W
                for q, blocks in enumerate((((0, 0),), ((P, 0), (2 * P, 1)))):
                    for i, (a, j) in enumerate(blocks):
                        last = pe.matmul(ps_n[q][:, o:o + W], prT[k % 2][:, a:a + P],
                                         vx[u][:, j, k, :, :].rearrange("p b d -> p (b d)"),
                                         start=(i == 0), stop=(i == len(blocks) - 1))
                last.then_inc(s_pn, 1)

            pe.wait_ge(s_one, 4)

            def step(n, u, front, heads, back):
                v = 1 - u
                m = n - 1
                for k in range(H):
                    ahead = head(n, u, k + 2, front, heads, back)
                    if ahead:
                        scores(*ahead)
                    if heads:
                        turned(n, u, k)
                    behind = head(n, u, k - 1, front, heads, back)
                    if behind:
                        weighted(*behind)
                    if front and k == 2:
                        after(pe, s_xn, n, -1, 2)
                        after(pe, s_x3T, n, 2)
                        turn(ps_a, xn[v]).then_inc(s_pxt, 1)
                    if front and k == 4:
                        after(pe, s_xT, n, -1)
                        after(pe, s_lg, n, 2)
                        product(ps_b, wT[:, 0], xT).then_inc(s_pq, 1)
                    if back and k == 6:
                        after(pe, s_o, m)
                        if front:
                            after(pe, s_xT, n, -1)
                        else:
                            after(pe, s_x3T, m, 1)
                        turn(ps_a, o).then_inc(s_pot, 1)
                    if back and k == 8:
                        after(pe, s_oT, m)
                        if front:
                            after(pe, s_qf, n, -1)
                        else:
                            after(pe, s_lg, m, 1)
                        product(ps_b, oT, wT[:, 1]).then_inc(s_po, 1)
                    if back and k == 12:
                        after(pe, s_xn3, m, 0, 2)
                        turn(ps_a, rows[v]).then_inc(s_px3, 1)
                    if back and k == 13:
                        after(pe, s_x3T, m)
                        after(pe, s_x3, m, 0, 2)
                        for j in range(2):
                            for c in range(C):
                                last = pe.matmul(ps_b[:, j * E:(j + 1) * E], x3T[:, c, j * P:(j + 1) * P],
                                                 wr[:, c, :], start=(c == 0), stop=(c == C - 1))
                        last.then_inc(s_plg, 1)

            pipeline(step)(pe)


def experts_choice(nc, S, ins, dram, keep, out):
    N, D, C, E, F, NT, CT = S.N, S.D, S.C, S.E, S.F1, S.NT, S.KT
    FC = -(-F // P)
    FULL = F // P
    LAST = F - FULL * P
    TAKE = S.K1
    G = ins["L1_ffn_W_up"].shape[0]
    GRP = P // E
    LEVELS = [26, 22, 18, 14, 10, 6, 2, 0]
    WS = 256.0
    FIRST = 4
    assert GRP == 16 and LAST and E // G == 2 and TAKE <= 512
    ident, ones, tg, prob = keep["ident"], keep["ones"], keep["tg"], keep["prob"]
    with ExitStack() as ctx:
        def sb(name, shape, dt=F32):
            return ctx.enter_context(nc.sbuf_tensor("d_" + name, shape, dt))

        def pb(name, shape):
            return ctx.enter_context(nc.psum_tensor("d_" + name, shape, F32))

        sem = stage_semaphores(nc, ctx, "d_")
        s_pass = sem("pass"); s_passd = sem("passd"); s_passs = sem("passs")

        tri = sb("tri", [P, P], F16)
        ones16 = sb("ones16", [P, P], F16)
        same = sb("same", [P, P], F16)
        lane = sb("lane", [P, P], F16)
        tile_no = sb("tile_no", [P, CT], F16)
        token1 = sb("token1", [P, NT])
        run_on = sb("run_on", [P, E, NT])
        lane_i = sb("lane_i", [P, 1], I32)
        try_i = sb("try_i", [P, 1], I32)
        tries = sb("tries", [P, len(LEVELS)], I32)
        bu_in = sb("bu_in", [FC * G, P])
        buT = sb("buT", [P, FC * G])
        bd = sb("bd", [P, E, D])

        spread = sb("spread", [P, NT, E, GRP])
        byexp = sb("byexp", [P, N])
        thr = sb("thr", [P, 1], I32)
        cand = sb("cand", [P, 1], I32)
        hit = sb("hit", [P, N], F16)
        cnt = sb("cnt", [P, 1])
        ok = sb("ok", [P, 1], F16)
        more = sb("more", [P, 1], I32)
        thr_row = sb("thr_row", [P, P])
        thr_e = sb("thr_e", [P, E])
        above = sb("above", [P, E, NT])
        tied = sb("tied", [P, E, NT])
        marks = [sb(f"marks{k}", [P, E, NT], F16) for k in range(3)]
        cum = sb("cum", [P, E, NT])
        excl = [sb(f"excl{k}", [P, E, NT], F16) for k in range(2)]
        room = sb("room", [P, E])
        fits = sb("fits", [P, E, NT])
        taken = sb("taken", [P, E, NT])
        pos = sb("pos", [P, E, NT])
        value = sb("value", [P, E, NT])
        slot = sb("slot", [P, E, NT], I32)
        slot_lo = sb("slot_lo", [P, E, NT], I32)
        slot_hi = sb("slot_hi", [P, E, NT], I32)
        lo16 = sb("lo16", [P, E, NT], F16)
        hi16 = sb("hi16", [P, E, NT], F16)

        at_lo = [sb(f"at_lo{u}", [P, NT, P], F16) for u in range(2)]
        at_hi = [sb(f"at_hi{u}", [P, NT, CT], F16) for u in range(2)]
        vhi = [sb(f"vhi{u}", [P, NT, CT], F16) for u in range(2)]
        g_idx = [sb(f"g_idx{u}", [P, CT], I32) for u in range(2)]
        s_idx = [sb(f"s_idx{u}", [P, CT], I32) for u in range(2)]
        who = sb("who", [P, E, CT])
        xg = [sb(f"xg{u}", [P, CT, S.ROW]) for u in range(2)]
        gate = [sb(f"gate{u}", [P, CT]) for u in range(2)]
        b1 = [sb(f"b1{u}", [P, FC]) for u in range(2)]
        xh = [sb(f"xh{u}", [P, C, TAKE], F16) for u in range(2)]
        xl = [sb(f"xl{u}", [P, C, TAKE], F16) for u in range(2)]
        w1 = sb("w1", [P, C, F])
        w2 = sb("w2", [P, FC, D])
        w1h = [sb(f"w1h{u}", [P, C, F], F16) for u in range(2)]
        w1l = [sb(f"w1l{u}", [P, C, F], F16) for u in range(2)]
        w2h = [sb(f"w2h{u}", [P, FC, D], F16) for u in range(2)]
        w2l = [sb(f"w2l{u}", [P, FC, D], F16) for u in range(2)]
        h = [sb(f"h{k}", [P, TAKE]) for k in range(2)]
        hh = sb("hh", [P, FC, TAKE], F16)
        hl = sb("hl", [P, FC, TAKE], F16)
        yb = sb("yb", [P, CT, D])
        y = sb("y", [P, CT, D])

        ps_t = pb("ps_t", [P, 4, 512])
        ps_y = [pb(f"ps_y{k}", [P, 512]) for k in range(2)]
        ps_i = pb("ps_i", [P, 512])
        ps_r = pb("ps_r", [P, 512])
        ps_h = [ps_t[:, k, :] for k in range(4)]
        ps_x = [ps_y[k][:, 0:C * P].rearrange("p (c t) -> p c t", c=C) for k in range(2)]

        s_cst = sem("cst"); s_byA = sem("byA"); s_abv = sem("abv"); s_si = sem("si"); s_ldb = sem("ldb")
        s_try = sem("try"); s_tries = sem("tries")
        s_spr = sem("spr"); s_pt = sem("pt"); s_bye = sem("bye"); s_thr = sem("thr"); s_cand = sem("cand")
        s_cnt = sem("cnt"); s_ok = sem("ok"); s_pok = sem("pok"); s_more = sem("more"); s_row = sem("row")
        s_prow = sem("prow"); s_thre = sem("thre"); s_cmp = sem("cmp"); s_in = sem("in"); s_cum = sem("cum")
        s_excl = sem("excl"); s_prank = sem("prank"); s_room = sem("room"); s_fits = sem("fits")
        s_tk1 = sem("tk1"); s_taken = sem("taken"); s_pos = sem("pos"); s_slot = sem("slot"); s_value = sem("value")
        s_split = sem("split"); s_lohi = sem("lohi"); s_pbu = sem("pbu"); s_buT = sem("buT"); s_fill = sem("fill")
        s_atlo = sem("atlo"); s_athi = sem("athi"); s_vhi = sem("vhi"); s_pidx = sem("pidx"); s_gi = sem("gi")
        s_g = [sem("g0"), sem("g1")]; s_w = sem("w"); s_gate = sem("gate"); s_b1 = sem("b1")
        s_px = sem("px"); s_xh = sem("xh"); s_xl = sem("xl"); s_wh = sem("wh"); s_wl = sem("wl")
        s_ph = sem("ph"); s_h = sem("h"); s_hh = sem("hh"); s_hl = sem("hl")
        s_py = sem("py"); s_yb = sem("yb"); s_y = sem("y"); s_add = sem("add")

        def pipeline(step):
            def run(eng):
                step(-2, 0, 0, True, False, False)
                step(-1, 1, 0, True, True, False)
                with eng.Fori(0, E // 2 - 1) as i:
                    step(i * 2, 0, i, True, True, True)
                    step(i * 2 + 1, 1, i + 1, True, True, True)
                step(E - 2, 0, G - 1, False, True, True)
                step(E - 1, 1, G, False, False, True)
            return run

        def count(eng, what, value):
            if not isinstance(value, int) or value > 0:
                eng.wait_ge(what, value)

        def wide(t):
            return t[:].rearrange("p a b -> p (a b)")

        def rows_of(f):
            return P if f < FULL else LAST

        block = ctx.enter_context(nc.Block())
        flat_out = out.rearrange("b t d -> (b t) d")

        @block.sync
        def _(sp):
            bu = ins["L1_ffn_b_up"]
            sp.wait_ge(s_fill, 2)
            sp.dma_start(bu_in[0:FULL * G, :], bu[:, 0:FULL * P].rearrange("g (c p) -> c g p", p=P)).then_inc(s_ldb, 16)
            sp.dma_start(bu_in[FULL * G:FC * G, 0:LAST], bu[:, FULL * P:F]).then_inc(s_ldb, 16)
            sp.dma_start(bd[:], ins["L1_ffn_b_down"].partition_broadcast(P)).then_inc(s_ldb, 16)

            def load(e, g):
                sp.dma_start(w1[:], ins["L1_ffn_W_up"][g].rearrange("(c p) f -> p c f", p=P)).then_inc(s_w, 16)
                down = ins["L1_ffn_W_down"][e]
                sp.dma_start(w2[:, 0:FULL, :], down[0:FULL * P, :].rearrange("(c p) d -> p c d", p=P))\
                    .then_inc(s_w, 16)
                sp.dma_start(w2[0:LAST, FULL, :], down[FULL * P:F, :]).then_inc(s_w, 16)

            load(0, 0)

            def step(e, u, g, slots, rows, products):
                if rows and not (isinstance(e, int) and e + 2 >= E):
                    sp.wait_ge(s_wl, (e + 2) * 2)
                    load(e + 2, g + 1 if u == 0 else g)

            pipeline(step)(sp)

        @block.gpsimd
        def _(pool):
            pool.memset(bu_in[:], 0.0).then_inc(s_fill, 1)
            pool.memset(w2[:], 0.0).then_inc(s_fill, 1)
            pool.memset(tri[:], 1.0).then_inc(s_cst, 1)
            pool.memset(ones16[:], 1.0).then_inc(s_cst, 1)
            pool.memset(run_on[:], 1.0).then_inc(s_cst, 1)
            pool.memset(same[:], 1.0).then_inc(s_cst, 1)
            pool.iota(lane[:], pattern=[[1, P]], base=0, channel_multiplier=0,
                      allow_small_or_imprecise_dtypes=True).then_inc(s_cst, 1)
            pool.iota(tile_no[:], pattern=[[1, CT]], base=0, channel_multiplier=0,
                      allow_small_or_imprecise_dtypes=True).then_inc(s_cst, 1)
            pool.iota(token1[:], pattern=[[P, NT]], base=1, channel_multiplier=1,
                      allow_small_or_imprecise_dtypes=True).then_inc(s_cst, 1)
            pool.iota(lane_i[:], pattern=[[0, 1]], base=0, channel_multiplier=1).then_inc(s_cst, 1)
            pool.wait_ge(s_cst, 8)
            pool.affine_select(out=tri[:], in_=tri[:], compare_op=ALU.is_ge, fill=0.0, base=0,
                               pattern=[[1, P]], channel_multiplier=-1).then_inc(s_cst, 1)
            pool.memset(run_on[:, :, 0], 0.0).then_inc(s_cst, 1)
            blocks = same[:].rearrange("p (a b) -> p a b", b=GRP)
            pool.affine_select(out=blocks, in_=blocks, compare_op=ALU.is_ge, fill=0.0, base=0,
                               pattern=[[-GRP, E], [0, GRP]], channel_multiplier=1).then_inc(s_cst, 1)
            pool.wait_ge(s_cst, 11)
            pool.affine_select(out=blocks, in_=blocks, compare_op=ALU.is_ge, fill=0.0, base=GRP - 1,
                               pattern=[[GRP, E], [0, GRP]], channel_multiplier=-1).then_inc(s_cst, 1)

            def step(e, u, g, slots, rows, products):
                v = 1 - u
                if rows:
                    pool.wait_ge(s_gi, (e + 2) * 2)
                    count(pool, s_px, e * CT)
                    count(pool, s_gate, e)
                    apart(pool, s_pass)
                    for j in range(CT):
                        pool.indirect_dma_start(
                            out=xg[v][:, j, :], out_offset=None, in_=dram["rows"],
                            in_offset=bass.IndirectOffsetOnAxis(ap=g_idx[v][:, j:j + 1], axis=0))\
                            .then_inc(s_g[v], 16)
                if products:
                    count(pool, s_add, e * CT * 16)
                    pool.wait_ge(s_si, e + 1)
                    for j in range(CT):
                        pool.wait_ge(s_y, e * CT + j + 1)
                        apart(pool, s_pass)
                        pool.indirect_dma_start(
                            out=flat_out, out_offset=bass.IndirectOffsetOnAxis(ap=s_idx[u][:, j:j + 1], axis=0),
                            in_=y[:, j, :], in_offset=None, compute_op=ALU.add).then_inc(s_add, 16)

            pipeline(step)(pool)
            pool.wait_ge(s_add, E * CT * 16)

        @block.scalar
        def _(act):
            act.wait_ge(s_pt, 2)
            for k in (1, 3):
                act.wait_ge(s_pt, k + 1)
                act.activation(byexp[:, k * 512:(k + 1) * 512], ps_t[:, k, :], ACT.Copy).then_inc(s_byA, 1)

            def step(e, u, g, slots, rows, products):
                v = 1 - u
                if products:
                    act.wait_ge(s_b1, e + 1)
                for f in range(FC):
                    r = rows_of(f)
                    if products:
                        act.wait_ge(s_ph, e * FC + f + 1)
                        count(act, s_hl, e * FC + f - 1 if f >= 2 else e * FC)
                        act.activation(h[f % 2][0:r, :], ps_h[f % 4][0:r, 0:TAKE], ACT.Silu,
                                       bias=b1[u][0:r, f:f + 1], scale=1.0 / WS).then_inc(s_h, 1)
                        act.wait_ge(s_h, e * FC + f + 1)
                        if f == 0:
                            count(act, s_py, e * CT)
                        act.activation(hh[0:r, f, :], h[f % 2][0:r, :], ACT.Copy).then_inc(s_hh, 1)
                    if rows and f in (0, 2):
                        if f == 0:
                            act.wait_ge(s_w, (e + 2) * 48)
                            count(act, s_py, e * CT)
                        stage, high = ((w1, w1h[v]), (w2, w2h[v]))[f // 2]
                        act.activation(high[:], stage[:], ACT.Copy, scale=WS).then_inc(s_wh, 1)
                    if rows and 0 <= f - FIRST < CT:
                        j = f - FIRST
                        act.wait_ge(s_px, (e + 1) * CT + j + 1)
                        act.activation(xh[v][:, :, j * P:(j + 1) * P], ps_x[j % 2], ACT.Copy).then_inc(s_xh, 1)
                if products:
                    for j in range(CT):
                        act.wait_ge(s_yb, e * CT + j + 1)
                        if j == 0:
                            count(act, s_add, e * CT * 16)
                        act.activation(y[:, j, :], yb[:, j, :], ACT.Copy, scale=gate[u][:, j:j + 1])\
                            .then_inc(s_y, 1)

            pipeline(step)(act)

        @block.vector
        def _(dve):
            dve.tensor_copy(spread[:], prob[:].unsqueeze(3).to_broadcast([P, NT, E, GRP])).then_inc(s_spr, 1)
            dve.wait_ge(s_cst, 12)
            dve.tensor_scalar(try_i[:], lane_i[:], GRP - 1, None, ALU.bitwise_and).then_inc(s_try, 1)
            dve.wait_ge(s_try, 1)
            for n, low in enumerate(LEVELS):
                if low:
                    dve.tensor_scalar(tries[:, n:n + 1], try_i[:], low, None, ALU.logical_shift_left)\
                        .then_inc(s_tries, 1)
                else:
                    dve.tensor_scalar(tries[:, n:n + 1], try_i[:], 2, None, ALU.logical_shift_right)\
                        .then_inc(s_tries, 1)
            for k in (0, 2):
                dve.wait_ge(s_pt, k + 1)
                dve.tensor_copy(byexp[:, k * 512:(k + 1) * 512], ps_t[:, k, :]).then_inc(s_bye, 1)
            dve.wait_ge(s_pbu, 1)
            dve.tensor_copy(buT[:], ps_i[:, 0:FC * G]).then_inc(s_buT, 1)
            dve.wait_ge(s_bye, 2)
            dve.wait_ge(s_byA, 2)
            dve.wait_ge(s_tries, len(LEVELS))
            for n, low in enumerate(LEVELS):
                if n == 0:
                    dve.tensor_copy(cand[:], tries[:, 0:1]).then_inc(s_cand, 1)
                else:
                    dve.wait_ge(s_thr, n)
                    dve.tensor_tensor(cand[:], thr[:], tries[:, n:n + 1], ALU.bitwise_or).then_inc(s_cand, 1)
                dve.wait_ge(s_cand, n + 1)
                dve.tensor_scalar(hit[:], byexp[:], cand[:].bitcast(F32), 0.0, ALU.is_ge, ALU.add,
                                  accum_out=cnt[:]).then_inc(s_cnt, 1)
                dve.wait_ge(s_cnt, n + 1)
                dve.tensor_scalar(ok[:], cnt[:], float(TAKE), None, ALU.is_ge).then_inc(s_ok, 1)
                dve.wait_ge(s_pok, n + 1)
                if low:
                    dve.tensor_scalar(more[:], ps_r[:, 0:1], -1.0, float(1 << low), ALU.add, ALU.mult)\
                        .then_inc(s_more, 1)
                else:
                    dve.tensor_scalar(more[:], ps_r[:, 0:1], 0.25, -1.0, ALU.mult, ALU.add).then_inc(s_more, 1)
                dve.wait_ge(s_more, n + 1)
                if n == 0:
                    dve.tensor_copy(thr[:], more[:]).then_inc(s_thr, 1)
                else:
                    dve.tensor_tensor(thr[:], thr[:], more[:], ALU.bitwise_or).then_inc(s_thr, 1)
            dve.wait_ge(s_thr, len(LEVELS))
            dve.tensor_copy(thr_row[:], thr[:].bitcast(F32).to_broadcast([P, P])).then_inc(s_row, 1)
            dve.wait_ge(s_prow, 1)
            dve.tensor_copy(thr_e[:], ps_r[:, 0:P].rearrange("p (e j) -> p e j", e=E)[:, :, 0]).then_inc(s_thre, 1)
            dve.wait_ge(s_thre, 1)
            bt = thr_e[:].unsqueeze(2).to_broadcast([P, E, NT])
            by_e = prob[:].rearrange("p i e -> p e i")
            dve.tensor_tensor(tied[:], by_e, bt, ALU.is_equal).then_inc(s_cmp, 1)
            dve.tensor_tensor(above[:], by_e, bt, ALU.is_gt).then_inc(s_cmp, 1)

            def rank(k, what):
                dve.tensor_copy(marks[k][:], what[:]).then_inc(s_in, 1)
                if k:
                    dve.wait_ge(s_excl, k)
                dve.tensor_tensor_scan(wide(cum), wide(run_on), wide(what), 0.0, ALU.mult, ALU.add)\
                    .then_inc(s_cum, 1)
                dve.wait_ge(s_cum, k + 1)
                dve.tensor_tensor(excl[k][:], cum[:], what[:], ALU.subtract).then_inc(s_excl, 1)
                dve.wait_ge(s_prank, k + 1)

            dve.wait_ge(s_cmp, 2)
            dve.tensor_copy(marks[2][:], above[:]).then_inc(s_abv, 1)
            rank(0, tied)
            dve.tensor_reduce(room[:], ps_r[:, 256:256 + E * NT].rearrange("p (e i) -> p e i", e=E), AX_X, ALU.add,
                              negate=True).then_inc(s_room, 1)
            dve.wait_ge(s_room, 1)
            dve.tensor_scalar(room[:], room[:], float(TAKE), None, ALU.add).then_inc(s_room, 1)
            dve.wait_ge(s_room, 2)
            dve.tensor_tensor(fits[:], ps_r[:, 0:E * NT].rearrange("p (e i) -> p e i", e=E),
                              room[:].unsqueeze(2).to_broadcast([P, E, NT]), ALU.is_le).then_inc(s_fits, 1)
            dve.wait_ge(s_fits, 1)
            dve.tensor_tensor(fits[:], fits[:], tied[:], ALU.mult).then_inc(s_tk1, 1)
            dve.wait_ge(s_tk1, 1)
            dve.tensor_tensor(taken[:], fits[:], above[:], ALU.add).then_inc(s_taken, 1)
            dve.wait_ge(s_taken, 1)
            rank(1, taken)
            dve.tensor_copy(pos[:], ps_r[:, 0:E * NT].rearrange("p (e i) -> p e i", e=E)).then_inc(s_pos, 1)
            dve.tensor_tensor(value[:], token1[:].unsqueeze(1).to_broadcast([P, E, NT]), taken[:], ALU.mult)\
                .then_inc(s_value, 1)
            dve.wait_ge(s_pos, 1)
            dve.tensor_scalar(slot[:], pos[:], -1.0, None, ALU.add).then_inc(s_slot, 1)
            dve.wait_ge(s_slot, 1)
            dve.tensor_scalar(slot_lo[:], slot[:], P - 1, None, ALU.bitwise_and).then_inc(s_split, 1)
            dve.tensor_scalar(slot_hi[:], slot[:], P.bit_length() - 1, None, ALU.arith_shift_right)\
                .then_inc(s_split, 1)
            dve.wait_ge(s_split, 2)
            dve.tensor_copy(lo16[:], slot_lo[:]).then_inc(s_lohi, 1)
            dve.tensor_copy(hi16[:], slot_hi[:]).then_inc(s_lohi, 1)
            dve.wait_ge(s_value, 1)
            dve.wait_ge(s_lohi, 2)
            dve.wait_ge(s_buT, 1)

            def of(table, e):
                return table[:, e, :] if isinstance(e, int) else \
                    table[:, bass.ds(e, 1), :].rearrange("p a b -> p (a b)")

            def step(e, u, g, slots, rows, products):
                v = 1 - u
                if slots:
                    count(dve, s_pidx, e + 1)
                    dve.tensor_tensor(at_lo[u][:], lane[:].unsqueeze(1).to_broadcast([P, NT, P]),
                                      of(lo16, e + 2).unsqueeze(2).to_broadcast([P, NT, P]), ALU.is_equal)\
                        .then_inc(s_atlo, 1)
                    dve.tensor_tensor(at_hi[u][:], tile_no[:].unsqueeze(1).to_broadcast([P, NT, CT]),
                                      of(hi16, e + 2).unsqueeze(2).to_broadcast([P, NT, CT]), ALU.is_equal)\
                        .then_inc(s_athi, 1)
                    dve.wait_ge(s_athi, e + 3)
                    dve.tensor_tensor(vhi[u][:], at_hi[u][:], of(value, e + 2).unsqueeze(2)
                                      .to_broadcast([P, NT, CT]), ALU.mult).then_inc(s_vhi, 1)
                for f in range(FC):
                    r = rows_of(f)
                    if products:
                        dve.wait_ge(s_hh, e * FC + f + 1)
                        dve.tensor_tensor(hl[0:r, f, :], h[f % 2][0:r, :], hh[0:r, f, :], ALU.subtract)\
                            .then_inc(s_hl, 1)
                    if rows and f in (1, 3):
                        stage, high, low = ((w1, w1h[v], w1l[v]), (w2, w2h[v], w2l[v]))[f // 2]
                        dve.wait_ge(s_wh, (e + 1) * 2 + f // 2 + 1)
                        dve.scalar_tensor_tensor(out=low[:], in0=stage[:], scalar=WS, in1=high[:], op0=ALU.mult,
                                                 op1=ALU.subtract).then_inc(s_wl, 1)
                    if rows and 0 <= f - FIRST < CT:
                        j = f - FIRST
                        dve.wait_ge(s_xh, (e + 1) * CT + j + 1)
                        dve.tensor_tensor(xl[v][:, :, j * P:(j + 1) * P], ps_x[j % 2],
                                          xh[v][:, :, j * P:(j + 1) * P], ALU.subtract).then_inc(s_xl, 1)
                if rows:
                    count(dve, s_y, e * CT)
                    dve.tensor_copy(gate[v][:], xg[v][:, :, D + e + 1] if isinstance(e, int) else
                                    xg[v][:, :, bass.ds(D + 1 + e, 1)].rearrange("p a b -> p (a b)"))\
                        .then_inc(s_gate, 1)
                    by_group = buT[:].rearrange("p (c g) -> p c g", g=G)
                    dve.tensor_copy(b1[v][:], by_group[:, :, g] if isinstance(g, int) else
                                    by_group[:, :, bass.ds(g, 1)].rearrange("p a b -> p (a b)")).then_inc(s_b1, 1)
                if slots:
                    dve.wait_ge(s_pidx, e + 3)
                    if not (isinstance(e, int) and e < 0):
                        dve.wait_ge(s_g[u], (e - u) * (8 * CT) + 16 * CT)
                    dve.tensor_scalar(g_idx[u][:], ps_i[:, 0:CT], -1.0, 0.0, ALU.add, ALU.max).then_inc(s_gi, 1)
                    dve.tensor_copy(of(who, e + 2), ps_i[:, 0:CT]).then_inc(s_gi, 1)
                if products:
                    count(dve, s_add, e * CT * 16)
                    dve.wait_ge(s_gi, (e + 1) * 2)
                    dve.tensor_scalar(s_idx[u][:], of(who, e), -1.0, 0.0, ALU.add, ALU.max).then_inc(s_si, 1)
                    for j in range(CT):
                        dve.wait_ge(s_py, e * CT + j + 1)
                        if j == 0:
                            count(dve, s_y, e * CT)
                        dve.scalar_tensor_tensor(out=yb[:, j, :], in0=ps_y[(j + CT) % 2][:, 0:D], scalar=1.0 / WS,
                                                 in1=of(bd, e), op0=ALU.mult, op1=ALU.add).then_inc(s_yb, 1)

            pipeline(step)(dve)

        @block.tensor
        def _(pe):
            pe.wait_ge(s_spr, 1)
            for i in range(NT):
                last = pe.transpose(ps_t[:, i // 4, (i % 4) * P:(i % 4 + 1) * P],
                                    spread[:, i, :, :].rearrange("p e j -> p (e j)"), ident[:])
                if i % 4 == 3:
                    last.then_inc(s_pt, 1)
            pe.wait_ge(s_ldb, 48)
            pe.transpose(ps_i[:, 0:FC * G], bu_in[:], ident[0:FC * G, 0:FC * G]).then_inc(s_pbu, 1)
            pe.wait_ge(s_cst, 12)
            for n in range(len(LEVELS)):
                pe.wait_ge(s_ok, n + 1)
                pe.matmul(ps_r[:, 0:1], same[:], ok[:], start=True, stop=True).then_inc(s_pok, 1)
            pe.wait_ge(s_row, 1)
            pe.transpose(ps_r[:, 0:P], thr_row[:], ident[:]).then_inc(s_prow, 1)
            pe.wait_ge(s_thre, 1)
            pe.wait_ge(s_abv, 1)
            pe.matmul(ps_r[:, 256:256 + E * NT], ones16[:], wide(marks[2]), start=True, stop=True)
            for k in range(2):
                pe.wait_ge(s_in, k + 1)
                if k:
                    pe.wait_ge(s_fits, 1)
                pe.matmul(ps_r[:, 0:E * NT], tri[:], wide(marks[k]), start=True, stop=False)
                pe.wait_ge(s_excl, k + 1)
                pe.matmul(ps_r[:, 0:E * NT], ones16[:], wide(excl[k]), start=False, stop=True).then_inc(s_prank, 1)
            pe.wait_ge(s_buT, 1)
            pe.wait_ge(s_bye, 2)
            pe.wait_ge(s_byA, 2)

            def step(e, u, g, slots, rows, products):
                v = 1 - u
                if products:
                    pe.wait_ge(s_xl, (e + 1) * CT)
                    pe.wait_ge(s_wl, (e + 1) * 2)
                for f in range(FC):
                    r = rows_of(f)
                    if products:
                        if f >= 4:
                            pe.wait_ge(s_h, e * FC + f - 3)
                        for c in range(C):
                            hi, lo = w1h[u][:, c, f * P:f * P + r], w1l[u][:, c, f * P:f * P + r]
                            for k, (a, b) in enumerate(((hi, xh[u]), (hi, xl[u]), (lo, xh[u]))):
                                last = pe.matmul(ps_h[f % 4][0:r, 0:TAKE], a, b[:, c, :],
                                                 start=(c == 0 and k == 0), stop=(c == C - 1 and k == 2))
                        last.then_inc(s_ph, 1)
                    if rows and 0 <= f - FIRST < CT:
                        j = f - FIRST
                        if j == 0:
                            pe.wait_ge(s_g[v], (e + 1 - v) * (8 * CT) + 16 * CT)
                            count(pe, s_yb, e * CT)
                        if j >= 2:
                            pe.wait_ge(s_xl, (e + 1) * CT + j - 1)
                        for c in range(C):
                            last = pe.transpose(ps_x[j % 2][:, c, :], xg[v][:, j, c * P:(c + 1) * P], ident[:])
                        last.then_inc(s_px, 1)
                if slots:
                    pe.wait_ge(s_vhi, e + 3)
                    pe.wait_ge(s_atlo, e + 3)
                    count(pe, s_gi, (e + 2) * 2)
                    for i in range(NT):
                        last = pe.matmul(ps_i[:, 0:CT], at_lo[u][:, i, :], vhi[u][:, i, :],
                                         start=(i == 0), stop=(i == NT - 1))
                    last.then_inc(s_pidx, 1)
                if products:
                    for j in range(CT):
                        if j >= 2:
                            pe.wait_ge(s_yb, e * CT + j - 1)
                        elif rows:
                            pe.wait_ge(s_xl, (e + 2) * CT + j - 1)
                        for f in range(FC):
                            r = rows_of(f)
                            if j == 0:
                                pe.wait_ge(s_hl, e * FC + f + 1)
                            hi, lo = hh[0:r, f, j * P:(j + 1) * P], hl[0:r, f, j * P:(j + 1) * P]
                            for k, (a, b) in enumerate(((hi, w2h[u]), (hi, w2l[u]), (lo, w2h[u]))):
                                last = pe.matmul(ps_y[(j + CT) % 2][:, 0:D], a, b[0:r, f, :],
                                                 start=(f == 0 and k == 0), stop=(f == FC - 1 and k == 2))
                        last.then_inc(s_py, 1)

            pipeline(step)(pe)


def build(nc, ins, out):
    S = Shapes(ins)
    dram = {
        "res": nc.dram_tensor("res", [S.N + S.CAP, S.D], F32).ap(),
        "rows": nc.dram_tensor("rows", [S.N, S.ROW], F32).ap(),
        "kT": nc.dram_tensor("kT", [S.B, 2, S.D, S.T], F16).ap(),
        "q": nc.dram_tensor("q", [2, 2, S.D, S.T], F16).ap(),
        "v": nc.dram_tensor("v", [S.B, P, S.TPB, S.D], F32).ap(),
    }
    with ExitStack() as ctx:
        ctx.enter_context(nc.allow_non_contiguous_dma(reason="bias vectors of a few hundred entries"))
        keep = {n: ctx.enter_context(nc.sbuf_tensor(n, s, F32)) for n, s in (
            ("ident", [P, P]), ("ones", [P, P]), ("zeros", [P, S.D]), ("tg", [P, 4]),
            ("wT_out", [P, 2, S.C, S.D]), ("match", [P, S.NT, S.E]),
            ("prob", [P, S.NT, S.E]), ("fallen", [P, S.NT]))}
        keep["fallen_n"] = ctx.enter_context(nc.sbuf_tensor("fallen_n", [P, 1], I32))
        attention_causal(nc, S, ins, dram, keep)
        experts_capacity(nc, S, ins, dram, keep)
        overflow_tokens(nc, S, ins, dram, keep)
        attention_dilated(nc, S, ins, dram, keep, out)
        experts_choice(nc, S, ins, dram, keep, out)


_INS = ["x", "ctx_1024", "g_xattn", "g_ffn", "L0_xattn_Wq", "L0_xattn_bq", "L0_xattn_Wk", "L0_xattn_bk",
        "L0_xattn_Wv", "L0_xattn_bv", "L0_xattn_Wff", "L0_xattn_bff", "L0_ffn_Wr", "L0_ffn_W1", "L0_ffn_b1",
        "L0_ffn_W2", "L0_ffn_b2", "L0_ffn_fw1", "L0_ffn_fb1", "L0_ffn_fw2", "L0_ffn_fb2", "L1_xattn_Wq",
        "L1_xattn_bq", "L1_xattn_Wk", "L1_xattn_bk", "L1_xattn_Wv", "L1_xattn_bv", "L1_xattn_Wo", "L1_xattn_bo",
        "L1_ffn_Wr", "L1_ffn_br", "L1_ffn_W_up", "L1_ffn_b_up", "L1_ffn_W_down", "L1_ffn_b_down"]


def kernel(**inputs):
    import numpy as _np
    import concourse.bacc as _bacc
    from concourse import mybir as _mybir
    from concourse.bass_utils import run_bass_kernel_spmd as _run

    nc = _bacc.Bacc("TRN2", target_bir_lowering=False, num_devices=1)
    arrays, aps = {}, {}
    for name in _INS:
        a = _np.ascontiguousarray(inputs[name])
        arrays[f"in_{name}_dram"] = a
        aps[name] = nc.dram_tensor(f"in_{name}_dram", a.shape, _mybir.dt.from_np(a.dtype), kind="ExternalInput").ap()
    out = nc.dram_tensor("out_0_dram", inputs["x"].shape, F32, kind="ExternalOutput").ap()
    build(nc, aps, out)
    r = _run(nc, [arrays], core_ids=[0])
    return r.results[0]["out_0_dram"]
```
